# Optimizing a Trainium2 kernel written in Bass

```python
import numpy as np
import jax
import jax.numpy as jnp

def _softmax(x, axis=-1):
    return jax.nn.softmax(x, axis=axis)

def _gelu(x):
    return jax.nn.gelu(x, approximate=True)

def _silu(x):
    return jax.nn.silu(x)

def _sigmoid(x):
    return jax.nn.sigmoid(x)

def _layernorm(x, axis=-1, eps=1e-05):
    m = jnp.mean(x, axis=axis, keepdims=True)
    v = jnp.var(x, axis=axis, keepdims=True)
    return (x - m) / jnp.sqrt(v + eps)

def _scatter_add(tgt, idx, src, axis=0):
    return tgt.at[idx].add(src)

def _segment_sum(src, seg, n):
    return jax.ops.segment_sum(src, seg, n)
kernel_name = 'mk_xattn_ffn_d1_seqx_r8_fc46c3'

def setup_inputs(seed: int=0):
    np.random.seed(seed)
    _w = jnp.asarray

    def _rec_inputs():
        import jax
        import jax.numpy as jnp
        _rk = jax.random.key(seed)
        x = -0.0005207 + 1.001 * jax.random.normal(jax.random.fold_in(_rk, 1), (32, 56, 512), jnp.float32)
        _lenS = 56 - jax.random.randint(jax.random.fold_in(_rk, 7), (32,), 0, max(1, 56 // 4) + 1, jnp.int32)
        _lenS2 = 1500 - jax.random.randint(jax.random.fold_in(_rk, 8), (32,), 0, max(1, 1500 // 4) + 1, jnp.int32)
        _ctx_4096P = jax.random.normal(jax.random.fold_in(_rk, 11), (32, 16, 512), jnp.float32)
        _ctx_4096c = jax.random.dirichlet(jax.random.fold_in(_rk, 511), 0.3 * jnp.ones((16,), jnp.float32), (32, 1500))
        _ctx_4096t = jnp.einsum('bsk,bkd->bsd', _ctx_4096c, _ctx_4096P)
        _ctx_4096t = _ctx_4096t * jax.lax.rsqrt(jnp.mean(jnp.square(_ctx_4096t)) + 1e-12) * 0.953939
        ctx_4096 = -0.00010331 + 0.999899 * (_ctx_4096t + 0.3 * jax.random.normal(jax.random.fold_in(_rk, 611), (32, 1500, 512), jnp.float32))
        return (x, ctx_4096)
    x, ctx_4096 = _rec_inputs()

    def _L0_xattn_setup():
        import jax, jax.numpy as jnp
        import numpy as np
        B, Q, D = (8, 64, 512)
        CTX = 512
        H, KV, HD = (16, 4, 96)
        G = H // KV
        key = jax.random.key(seed)
        ks = jax.random.split(key, 6)
        s = 0.02
        return {'latents': jax.random.normal(ks[0], (B, Q, D), jnp.float32), 'context': jax.random.normal(ks[1], (B, CTX, D), jnp.float32), 'Wq': jax.random.normal(ks[2], (H * HD, D), jnp.float32) * s, 'Wk': jax.random.normal(ks[3], (KV * HD, D), jnp.float32) * s, 'Wv': jax.random.normal(ks[4], (KV * HD, D), jnp.float32) * s, 'Wo': jax.random.normal(ks[5], (D, H * HD), jnp.float32) * s}
    _L0_xattn_all = _L0_xattn_setup()
    _L0_xattn_in = {k: v for k, v in _L0_xattn_all.items() if k in ('Wq', 'Wk', 'Wv', 'Wo')}
    del _L0_xattn_all

    def _L0_ffn_setup():
        import jax, jax.numpy as jnp
        import numpy as np
        TOP_K = 2
        key = jax.random.key(seed)
        k0, k1, k2 = jax.random.split(key, 3)
        B, S, D, H, E = (4, 256, 512, 512, 8)
        sc = 1.0 / np.sqrt(D).astype(np.float32)
        x = jax.random.normal(k0, (B, S, D), dtype=jnp.float32)
        W_gate = jax.random.normal(k1, (D, E), dtype=jnp.float32) * sc
        b_gate = jnp.zeros((E,), dtype=jnp.float32)
        W_e = jax.random.normal(k2, (E, D, H), dtype=jnp.float32) * sc
        b_e = jnp.zeros((E, H), dtype=jnp.float32)
        return {'x': x, 'W_gate': W_gate, 'b_gate': b_gate, 'W_e': W_e, 'b_e': b_e}
    _L0_ffn_all = _L0_ffn_setup()
    _L0_ffn_in = {k: v for k, v in _L0_ffn_all.items() if k in ('W_gate', 'b_gate', 'W_e', 'b_e')}
    del _L0_ffn_all
    return {'x': x, 'ctx_4096': ctx_4096, 'L0_xattn_Wq': _L0_xattn_in['Wq'], 'L0_xattn_Wk': _L0_xattn_in['Wk'], 'L0_xattn_Wv': _L0_xattn_in['Wv'], 'L0_xattn_Wo': _L0_xattn_in['Wo'], 'L0_ffn_W_gate': _L0_ffn_in['W_gate'], 'L0_ffn_b_gate': _L0_ffn_in['b_gate'], 'L0_ffn_W_e': _L0_ffn_in['W_e'], 'L0_ffn_b_e': _L0_ffn_in['b_e']}

def reference(x, ctx_4096, L0_xattn_Wq, L0_xattn_Wk, L0_xattn_Wv, L0_xattn_Wo, L0_ffn_W_gate, L0_ffn_b_gate, L0_ffn_W_e, L0_ffn_b_e):
    import jax
    import jax.numpy as jnp

    def _L0_xattn_ref(latents, context, Wq, Wk, Wv, Wo):
        import jax, jax.numpy as jnp
        import numpy as np
        B, Q, D = (8, 64, 512)
        CTX = 512
        H, KV, HD = (16, 4, 96)
        G = H // KV
        b, q_len, _ = latents.shape
        hidden = jnp.concatenate([context, latents], axis=1)
        s_len = hidden.shape[1]
        q = (latents @ Wq.T).reshape(b, q_len, H, HD)
        k = (hidden @ Wk.T).reshape(b, s_len, KV, HD)
        v = (hidden @ Wv.T).reshape(b, s_len, KV, HD)
        q = q.transpose(0, 2, 1, 3).reshape(b, KV, G, q_len, HD)
        k = k.transpose(0, 2, 1, 3)
        v = v.transpose(0, 2, 1, 3)
        scale = 1.0 / jnp.sqrt(jnp.asarray(HD, q.dtype))
        scores = jnp.einsum('bkgqd,bksd->bkgqs', q, k) * scale
        attn = jax.nn.softmax(scores.astype(jnp.float32), axis=-1).astype(q.dtype)
        out = jnp.einsum('bkgqs,bksd->bkgqd', attn, v)
        out = out.reshape(b, H, q_len, HD).transpose(0, 2, 1, 3).reshape(b, q_len, H * HD)
        return out @ Wo.T

    def _L0_ffn_ref(x, W_gate, b_gate, W_e, b_e):
        import jax, jax.numpy as jnp
        import numpy as np
        TOP_K = 2
        logits = x @ W_gate + b_gate
        _, top_idx = jax.lax.top_k(logits, TOP_K)
        y_all = jax.nn.relu(jnp.einsum('bsd,edh->bseh', x, W_e) + b_e)
        y = jnp.take_along_axis(y_all, top_idx[..., None], axis=2)
        return y.mean(axis=2)
    x = x + _L0_xattn_ref(_layernorm(x, axis=-1), ctx_4096, L0_xattn_Wq, L0_xattn_Wk, L0_xattn_Wv, L0_xattn_Wo)
    x = x + _L0_ffn_ref(_layernorm(x, axis=-1), L0_ffn_W_gate, L0_ffn_b_gate, L0_ffn_W_e, L0_ffn_b_e)
    return x

_drawn_inputs = setup_inputs


def setup_inputs(seed=0):
    import zlib

    import numpy as np

    out = dict(_drawn_inputs(seed))
    spreads = {'L0_ffn_b_gate': (0.0, 0.1), 'L0_ffn_b_e': (0.0, 0.1)}
    factors = {}
    for name, (base, spread) in spreads.items():
        noise = np.random.default_rng([zlib.crc32(name.encode()), seed]).standard_normal(out[name].shape)
        drawn = base * np.exp(spread * noise) if base else spread * noise
        out[name] = jnp.asarray(drawn.astype(out[name].dtype))
    for name, factor in factors.items():
        out[name] = (out[name] * factor).astype(out[name].dtype)
    return out
```

```python
from contextlib import ExitStack

import concourse.bass as bass
from concourse import mybir

F32 = mybir.dt.float32
F32R = mybir.dt.float32r
U32 = mybir.dt.uint32
ALU = mybir.AluOpType
ACT = mybir.ActivationFunctionType
AX = mybir.AxisListType

P = 128
B, Q, D = 32, 56, 512
S = 1500
H, KV, HD = 16, 4, 96
G = H // KV
E = 8
EPS = 1e-5
SCALE = float(HD) ** -0.5
KT = D // P
ROWS = B * Q
SL = S + Q
GQ = G * Q
KD = KV * HD
HH = H * HD

PIECE = P - HD
KTILES = KD // P
CHUNKS = 3
CS = S // CHUNKS
HALVES_C = 2
KH = KT // HALVES_C
LOADS = CHUNKS * HALVES_C
RAW = 3
VT = 125
VTC = CS // VT
NVT = S // VT

GROUPS = 4
GR = ROWS // GROUPS
RT = 112
GT = GR // RT
MQ = HH // P
MK = MQ + KTILES
NOUT = MK + GT
GB = GR // Q

HALVES = 2 * KV
HALF = GQ // 2
MAXCOLS = [(0, 390), (780, 388)]
PARTS = 2 * HALVES
UNITS = 7
NU = KV * UNITS
SBANKS = 4
AHEAD = 3
PRING = 4
NPROJ = CHUNKS * KTILES + NVT

OT = ROWS // P
HT = HH // P
HEAD_PIECES = [(0, 0, 96, 0), (0, 96, 32, 1), (1, 0, 64, 1), (1, 64, 64, 2), (2, 0, 32, 2), (2, 32, 96, 3)]


def wait_apart(eng, sem, value, waited):
    eng.wait_ge(sem, value)
    eng.sem_inc(waited, 1)


def f(ap):
    return ap.bitcast(F32)


def project(nc, w, io, scratch):
    with ExitStack() as ctx:
        sb = lambda name, shape, dt=F32: ctx.enter_context(nc.sbuf_tensor(name, shape, dt))
        sem = lambda name: ctx.enter_context(nc.semaphore(name))
        wq_raw = sb("wq_raw", [P, KT, HH])
        wkv_raw = sb("wkv_raw", [P, 2, KT, KD])
        wq = [sb(f"wq_{n}", [P, KT, HH], F32R) for n in ("hi", "lo")]
        x = sb("x_group", [RT, GT, D])
        xn = sb("x_normed", [RT, GT, D])
        stats = sb("ln_stats", [RT, GT, 6])
        mv = sb("ln_mean_var", [RT, GT, 2])
        std = sb("ln_std", [RT, GT])
        rstd = sb("ln_rstd", [RT, GT])
        eps = sb("eps_p", [P, 1])
        ident = sb("ident_p", [P, P])
        xt = [sb(f"xt_{n}", [P, KT, GR], F32R) for n in ("hi", "lo")]
        out = [sb(f"proj_out_{n}", [P, 2, GR], F32R) for n in ("hi", "lo")]
        pt = [ctx.enter_context(nc.psum_tensor(f"ps_xt{i}", [P, GR], F32)) for i in range(KT)]
        po = [ctx.enter_context(nc.psum_tensor(f"ps_out{i}", [P, GR], F32)) for i in range(4)]

        waited = sem("waited_p")
        x_loaded = sem("x_loaded")
        w_loaded = [sem(f"w_loaded{i}") for i in range(3)]
        consts = sem("consts_ready")
        stats_done, mv_done, std_done, rstd_done = sem("stats_done"), sem("mv_done"), sem("std_done"), sem("rstd_done")
        normed = sem("normed")
        turned = sem("turned")
        xt_hi, xt_lo = sem("xt_hi_ready"), sem("xt_lo_ready")
        w_hi, w_lo = sem("w_hi_ready"), sem("w_lo_ready")
        out_done = sem("out_done")
        out_hi, out_lo = sem("out_hi_ready"), sem("out_lo_ready")
        stored = [sem(f"stored{i}") for i in range(2)]
        xg = io["x"].rearrange("(g t r) d -> g r t d", t=GT, r=RT)
        qk_d = [s.rearrange("(g b) m q -> g m b q", b=GB) for s in scratch["qk"]]
        v_d = [s.rearrange("(g t r) n -> g t r n", t=GT, r=RT) for s in scratch["v"]]

        def uses(i):
            return len(range(i, NOUT, 2))

        with nc.Block() as block:
            @block.sync
            def _(sp):
                sp.dma_start(x[:], xg[0]).then_inc(x_loaded, 16)
                sp.dma_start(wq_raw[:, :, 0:HH // 2], io["wq"][:, :, 0:HH // 2]).then_inc(w_loaded[0], 16)
                sp.dma_start(wq_raw[:, :, HH // 2:], io["wq"][:, :, HH // 2:]).then_inc(w_loaded[1], 16)
                sp.dma_start(wkv_raw[:, 0], io["wk"]).then_inc(w_loaded[2], 16)
                sp.dma_start(wkv_raw[:, 1], io["wv"]).then_inc(w_loaded[2], 16)

                def group(g, more):
                    if more:
                        sp.wait_ge(normed, g * GT + GT)
                        sp.dma_start(x[:], xg[g + 1]).then_inc(x_loaded, 16)
                    for n in range(NOUT):
                        sp.wait_ge(out_lo, g * NOUT + n + 1)
                        for i in range(2):
                            if n < MK:
                                src = f(out[i][:, n % 2, :]).rearrange("p (b q) -> p b q", q=Q)
                                dst = qk_d[i][g, n * P:(n + 1) * P]
                            else:
                                src, dst = f(out[i][0:RT, n % 2, 0:KD]), v_d[i][g, n - MK]
                            sp.dma_start(dst, src).then_inc(stored[n % 2], 16)

                with sp.Fori(0, GROUPS - 1) as g:
                    group(g, True)
                group(GROUPS - 1, False)
                for i in range(2):
                    sp.wait_ge(stored[i], 32 * GROUPS * uses(i))

            @block.gpsimd
            def _(pool):
                pool.memset(eps[:], EPS).then_inc(consts, 1)
                pool.memset(ident[:], 0.0).then_inc(consts, 1)
                pool.wait_ge(consts, 2)
                pool.affine_select(out=ident[:], in_=ident[:], compare_op=ALU.not_equal, fill=1.0, base=0,
                                   pattern=[[-1, P]], channel_multiplier=1).then_inc(consts, 1)

            @block.scalar
            def _(act):
                def norm_scale(g):
                    act.wait_ge(mv_done, g * GT + GT)
                    act.activation(std[:], mv[:, :, 1], ACT.Sqrt, bias=eps[0:RT]).then_inc(std_done, 1)

                def split_out(g, n):
                    act.wait_ge(out_done, g * NOUT + n + 1)
                    act.wait_ge(stored[n % 2], g * (32 * uses(n % 2)) + 32 * (n // 2))
                    R, N = (P, GR) if n < MK else (RT, KD)
                    act.copy(out[0][0:R, n % 2, 0:N], po[n % 4][0:R, 0:N]).then_inc(out_hi, 1)

                def turn(g):
                    for k in range(KT):
                        act.wait_ge(turned, g * KT + k + 1)
                        if k == 0:
                            act.wait_ge(out_done, g * NOUT)
                        act.copy(xt[0][:, k, :], pt[k][:]).then_inc(xt_hi, 1)

                act.wait_ge(consts, 3)
                norm_scale(0)
                for i in range(2):
                    act.wait_ge(w_loaded[i], 16)
                    h = slice(i * HH // 2, (i + 1) * HH // 2)
                    act.copy(wq[0][:, :, h], wq_raw[:, :, h]).then_inc(w_hi, 1)
                    if i == 0:
                        turn(0)
                act.wait_ge(w_loaded[2], 32)
                act.copy(w["wk"][0][:], wkv_raw[:, 0]).then_inc(w_hi, 1)
                act.copy(w["wv"][0][:], wkv_raw[:, 1]).then_inc(w_hi, 1)

                def group(g, more):
                    for n in range(NOUT):
                        split_out(g, n)
                        if n == 8 and more:
                            norm_scale(g + 1)
                    if more:
                        turn(g + 1)

                with act.Fori(0, GROUPS - 1) as g:
                    group(g, True)
                group(GROUPS - 1, False)

            @block.vector
            def _(dve):
                def moments(g):
                    dve.wait_ge(x_loaded, g * 16 + 16)
                    for t in range(GT):
                        dve.bn_stats(stats[:, t, :], x[:, t, :]).then_inc(stats_done, 1)
                    for t in range(GT):
                        wait_apart(dve, stats_done, g * GT + t + 1, waited)
                        dve.bn_aggr(mv[:, t, :], stats[:, t, :]).then_inc(mv_done, 1)

                def norm(g):
                    dve.wait_ge(std_done, g + 1)
                    dve.wait_ge(turned, g * KT)
                    dve.reciprocal(rstd[:], std[:]).then_inc(rstd_done, 1)
                    dve.wait_ge(rstd_done, g + 1)
                    for t in range(GT):
                        dve.tensor_scalar(xn[:, t, :], x[:, t, :], mv[:, t, 0:1], rstd[:, t:t + 1],
                                          ALU.subtract, ALU.mult).then_inc(normed, 1)

                def split_out(g, n):
                    dve.wait_ge(out_hi, g * NOUT + n + 1)
                    R, N = (P, GR) if n < MK else (RT, KD)
                    dve.tensor_tensor(out[1][0:R, n % 2, 0:N], po[n % 4][0:R, 0:N], f(out[0][0:R, n % 2, 0:N]),
                                      ALU.subtract).then_inc(out_lo, 1)

                def turn(g):
                    for k in range(KT):
                        dve.wait_ge(xt_hi, g * KT + k + 1)
                        dve.tensor_tensor(xt[1][:, k, :], pt[k][:], f(xt[0][:, k, :]), ALU.subtract).then_inc(xt_lo, 1)

                moments(0)
                norm(0)
                for i in range(2):
                    dve.wait_ge(w_hi, i + 1)
                    h = slice(i * HH // 2, (i + 1) * HH // 2)
                    dve.tensor_tensor(wq[1][:, :, h], wq_raw[:, :, h], f(wq[0][:, :, h]), ALU.subtract).then_inc(w_lo, 1)
                    if i == 0:
                        turn(0)
                for i, name in enumerate(("wk", "wv")):
                    dve.wait_ge(w_hi, 3 + i)
                    dve.tensor_tensor(w[name][1][:], wkv_raw[:, i], f(w[name][0][:]), ALU.subtract).then_inc(w_lo, 1)

                def group(g, more):
                    for n in range(NOUT):
                        split_out(g, n)
                        if n == 6 and more:
                            moments(g + 1)
                        if n == 10 and more:
                            norm(g + 1)
                    if more:
                        turn(g + 1)

                with dve.Fori(0, GROUPS - 1) as g:
                    group(g, True)
                group(GROUPS - 1, False)

            @block.tensor
            def _(pe):
                pe.wait_ge(consts, 3)

                def turn(g):
                    pe.wait_ge(normed, g * GT + GT)
                    pe.wait_ge(xt_lo, g * KT)
                    for k in range(KT):
                        for t in range(GT):
                            mm = pe.transpose(pt[k][:, t * RT:(t + 1) * RT], xn[:, t, k * P:(k + 1) * P], ident[0:RT, 0:RT])
                        mm.then_inc(turned, 1)

                def product(g, n):
                    if n < 4:
                        pe.wait_ge(out_lo, g * NOUT)
                    else:
                        pe.wait_ge(out_lo, g * NOUT + n - 3)
                    last = 3 * KT - 1
                    for j in range(3 * KT):
                        k, (a, b) = j // 3, ((0, 0), (0, 1), (1, 0))[j % 3]
                        if n < MK:
                            stat = wq[a][:, k, n * P:(n + 1) * P] if n < MQ else w["wk"][a][:, k, (n - MQ) * P:(n - MQ + 1) * P]
                            mm = pe.matmul(po[n % 4][:, :], stat, xt[b][:, k, :], start=(j == 0), stop=(j == last))
                        else:
                            t = n - MK
                            mm = pe.matmul(po[n % 4][0:RT, 0:KD], xt[a][:, k, t * RT:(t + 1) * RT], w["wv"][b][:, k, :],
                                           start=(j == 0), stop=(j == last))
                    mm.then_inc(out_done, 1)

                def group(g):
                    turn(g)
                    pe.wait_ge(xt_lo, g * KT + KT)
                    for n in range(NOUT):
                        need = {0: 1, MQ // 2: 2, MQ: 4}.get(n)
                        if need:
                            pe.wait_ge(w_lo, need)
                        product(g, n)

                with pe.Fori(0, GROUPS) as g:
                    group(g)


def attend(nc, w, io, scratch):
    with ExitStack() as ctx:
        sb = lambda name, shape, dt=F32: ctx.enter_context(nc.sbuf_tensor(name, shape, dt))
        sem = lambda name: ctx.enter_context(nc.semaphore(name))
        raw = sb("ctx_raw", [P, RAW, KH, CS])
        ct = [sb(f"ctx_{n}", [P, CHUNKS, KT, CS], F32R) for n in ("hi", "lo")]
        kt = [sb("keys_hi", [HD, KV, SL], F32R), sb("keys_lo", [HD + 1, KV, SL], F32R)]
        vt_hi = sb("values_hi", [VT, NVT + 1, KV, HD + 1], F32R)
        vt_lo = sb("values_lo", [VT, NVT + 1, KV, HD], F32R)
        q = [sb("queries_hi", [HD + 1, KV * GQ], F32R), sb("queries_lo", [HD, KV * GQ], F32R)]
        pr = sb("probs", [VT, 2, 2 * GQ])
        prs = [sb(f"probs_{n}", [VT, PRING, 2 * GQ], F32R) for n in ("hi", "lo")]
        mpart = sb("max_parts", [HALF, HALVES, 2])
        mrow = sb("max_rows", [HALF, HALVES])
        mdiag = prs[1][0:HALF, 0:2, 0:KV * HALF]
        negident = sb("neg_ident", [HALF, HALF])
        ones = sb("ones_a", [HALF, P], F32R)
        osb = sb("attended", [HD + 1, 2, GQ])
        pproj = [ctx.enter_context(nc.psum_tensor(f"ps_proj{i}", [P, 512], F32)) for i in range(2)]
        psc = ctx.enter_context(nc.psum_tensor("ps_scores", [P, SBANKS, 512], F32))
        pav = ctx.enter_context(nc.psum_tensor("ps_attended", [P, 2, 512], F32))

        ctx_loaded = [sem(f"ctx_loaded{i}") for i in range(RAW)]
        qk_loaded, v_loaded = sem("qk_loaded"), sem("v_loaded")
        cleared = sem("ident_cleared")
        consts = sem("consts_ready_a")
        ctx_hi, ctx_lo = sem("ctx_hi_ready"), sem("ctx_lo_ready")
        proj_done = sem("proj_done")
        proj_hi, proj_lo = sem("proj_hi_ready"), sem("proj_lo_ready")
        maxmm_done, max_done = sem("max_scores_done"), sem("max_done")
        mrow_done, mdiag_done, mb_done, mneg_done = sem("max_rows_done"), sem("max_diag_done"), sem("max_spread"), sem("max_in_queries")
        scores_done, exp_done, p_hi, p_lo = sem("scores_done"), sem("exp_done"), sem("p_hi_ready"), sem("p_lo_ready")
        pv_done = sem("pv_done")
        o_copied, z_done = sem("o_copied"), sem("z_inverted")
        stored = [sem(f"att_stored{i}") for i in range(2)]

        qk_d = scratch["qk"]
        att_d = scratch["att"].rearrange("(h d) (b q) -> b d h q", d=HD, q=Q)
        rz_d = scratch["rz"].rearrange("h (b q) -> b h q", q=Q)

        with nc.Block() as block:
            @block.sync
            def _(sp):
                def load_qk(b):
                    for i in range(2):
                        sp.dma_start(f(q[i][0:HD, :]).rearrange("d (h q) -> d h q", q=Q),
                                     qk_d[i][b, 0:HH].rearrange("(h d) q -> d h q", d=HD)).then_inc(qk_loaded, 16)
                        rows = qk_d[i][b, HH:HH + KD].rearrange("(i r) q -> i r q", r=P)
                        sp.dma_start(f(kt[i][0:HD, 0:KTILES, S:SL]),
                                     rows[:, 0:HD].rearrange("i r q -> r i q")).then_inc(qk_loaded, 16)
                        for j in range(KTILES):
                            sp.dma_start(f(kt[i][j * PIECE:(j + 1) * PIECE, KTILES, S:SL]),
                                         rows[j, HD:P]).then_inc(qk_loaded, 16)

                def load_v(b):
                    for i, dst in enumerate((vt_hi[0:Q, NVT, :, 0:HD], vt_lo[0:Q, NVT])):
                        sp.dma_start(f(dst), scratch["v"][i].rearrange("(b q) (h d) -> b q h d", q=Q, d=HD)[b]).then_inc(v_loaded, 16)

                def store(b):
                    for h in range(KV):
                        sp.wait_ge(o_copied, b * KV + h + 1)
                        sp.dma_start(att_d[b, :, h * G:(h + 1) * G, :],
                                     osb[0:HD, h % 2, :].rearrange("d (h q) -> d h q", q=Q)).then_inc(stored[h % 2], 16)
                        sp.wait_ge(z_done, b * KV + h + 1)
                        sp.dma_start(rz_d[bass.ds(b, 1), h * G:(h + 1) * G, :],
                                     osb[HD:HD + 1, h % 2, :].rearrange("d (h q) -> d h q", q=Q)).then_inc(stored[h % 2], 16)

                def load_ctx(b, n):
                    if not (isinstance(b, int) and n < RAW):
                        sp.wait_ge(ctx_lo, b * LOADS + n - RAW + 1)
                    k = n % HALVES_C * KH
                    sp.dma_start(raw[:, n % RAW], io["ctx"][b, n // HALVES_C, :, k:k + KH, :]).then_inc(ctx_loaded[n % RAW], 16)

                for n in range(RAW):
                    load_ctx(0, n)
                load_qk(0)
                load_v(0)
                for n in range(RAW, LOADS):
                    load_ctx(0, n)
                with sp.Fori(0, B - 1) as b:
                    for n in range(LOADS):
                        load_ctx(b + 1, n)
                    store(b)
                    sp.wait_ge(scores_done, b * NU + NU)
                    load_qk(b + 1)
                    sp.wait_ge(pv_done, b * NU + NU)
                    load_v(b + 1)
                store(B - 1)
                for i in range(2):
                    sp.wait_ge(stored[i], B * KV // 2 * 32)

            @block.gpsimd
            def _(pool):
                pool.memset(negident[:], 0.0).then_inc(cleared, 1)
                pool.wait_ge(cleared, 1)
                pool.affine_select(out=negident[:], in_=negident[:], compare_op=ALU.not_equal, fill=-1.0, base=0,
                                   pattern=[[-1, HALF]], channel_multiplier=1).then_inc(consts, 1)

                def split_lo(b, n):
                    pool.wait_ge(ctx_hi, b * LOADS + n + 1)
                    c, k = n // HALVES_C, n % HALVES_C * KH
                    pool.tensor_tensor(ct[1][:, c, k:k + KH], raw[:, n % RAW], f(ct[0][:, c, k:k + KH]),
                                       ALU.subtract).then_inc(ctx_lo, 1)

                with pool.Fori(0, B) as b:
                    for n in range(LOADS):
                        split_lo(b, n)

            @block.scalar
            def _(act):
                def split_ctx(b, c):
                    for n in range(c * HALVES_C, (c + 1) * HALVES_C):
                        act.wait_ge(ctx_loaded[n % RAW], b * 32 + n // RAW * 16 + 16)
                        k = n % HALVES_C * KH
                        act.copy(ct[0][:, c, k:k + KH], raw[:, n % RAW]).then_inc(ctx_hi, 1)

                def keys(b, c, i):
                    s = slice(c * CS, (c + 1) * CS)
                    n = c * KTILES + i
                    act.wait_ge(proj_done, b * NPROJ + n + 1)
                    act.copy(kt[0][0:HD, i, s], pproj[n % 2][0:HD, 0:CS])
                    act.copy(kt[0][i * PIECE:(i + 1) * PIECE, KTILES, s], pproj[n % 2][HD:P, 0:CS]).then_inc(proj_hi, 1)

                def values(b, t):
                    n = CHUNKS * KTILES + t
                    act.wait_ge(proj_done, b * NPROJ + n + 1)
                    act.copy(vt_hi[:, t, :, 0:HD], pproj[n % 2][0:VT, 0:KD].rearrange("p (h d) -> p h d", d=HD)).then_inc(proj_hi, 1)

                def exp(b, u):
                    j = u % UNITS
                    R, N = (VT, 2 * GQ) if j < UNITS - 1 else (Q, GQ)
                    act.wait_ge(scores_done, b * NU + u + 1)
                    act.wait_ge(p_lo, b * NU + max(u - 1, 0))
                    act.activation(pr[0:R, u % 2, 0:N], psc[0:R, u % SBANKS, 0:N], ACT.Exp, scale=SCALE).then_inc(exp_done, 1)

                def probs_hi(b, u):
                    j = u % UNITS
                    R, N = (VT, 2 * GQ) if j < UNITS - 1 else (Q, GQ)
                    act.wait_ge(exp_done, b * NU + u + 1)
                    act.wait_ge(pv_done, b * NU + max(u - PRING + 1, 0))
                    act.copy(prs[0][0:R, u % PRING, 0:N], pr[0:R, u % 2, 0:N]).then_inc(p_hi, 1)

                def take_out(b, h):
                    act.wait_ge(pv_done, b * NU + (h + 1) * UNITS)
                    act.wait_ge(stored[h % 2], b * 64 + 32 * (h // 2))
                    act.copy(osb[0:HD, h % 2, :], pav[0:HD, h % 2, 0:GQ]).then_inc(o_copied, 1)

                def batch(b, more):
                    for c in range(CHUNKS):
                        for i in range(KTILES):
                            keys(b, c, i)
                    for t in range(NVT):
                        values(b, t)
                        if more and t in (4, 8):
                            act.wait_ge(proj_done, b * NPROJ + CHUNKS * KTILES + t)
                            split_ctx(b + 1, t // VTC - 1)
                    act.wait_ge(mb_done, b + 1)
                    act.copy(q[0][HD:HD + 1, :], pav[HD:HD + 1, :, 0:KV * HALF]).then_inc(mneg_done, 1)
                    for u in range(NU + 1):
                        if u < NU:
                            exp(b, u)
                        if u >= 1:
                            probs_hi(b, u - 1)
                        if u == 2 and more:
                            act.wait_ge(proj_done, b * NPROJ + NPROJ)
                            split_ctx(b + 1, 2)
                        if u >= 9 and (u - 9) % UNITS == AHEAD - 2:
                            take_out(b, (u - 9) // UNITS)
                    take_out(b, KV - 1)

                for c in range(CHUNKS):
                    split_ctx(0, c)
                with act.Fori(0, B - 1) as b:
                    batch(b, True)
                batch(B - 1, False)

            @block.vector
            def _(dve):
                dve.memset(f(ones[:]), 1.0).then_inc(consts, 1)
                dve.memset(f(vt_hi[:, :, :, HD:HD + 1]), 1.0).then_inc(consts, 1)
                dve.memset(f(kt[1][HD:HD + 1]), 1.0).then_inc(consts, 1)
                dve.wait_ge(consts, 4)

                def keys(b, c, i):
                    s = slice(c * CS, (c + 1) * CS)
                    n = c * KTILES + i
                    dve.wait_ge(proj_hi, b * NPROJ + n + 1)
                    dve.tensor_tensor(kt[1][0:HD, i, s], pproj[n % 2][0:HD, 0:CS], f(kt[0][0:HD, i, s]), ALU.subtract)
                    piece = slice(i * PIECE, (i + 1) * PIECE)
                    dve.tensor_tensor(kt[1][piece, KTILES, s], pproj[n % 2][HD:P, 0:CS], f(kt[0][piece, KTILES, s]),
                                      ALU.subtract).then_inc(proj_lo, 1)

                def values(b, t):
                    n = CHUNKS * KTILES + t
                    dve.wait_ge(proj_hi, b * NPROJ + n + 1)
                    dve.tensor_tensor(vt_lo[:, t], pproj[n % 2][0:VT, 0:KD].rearrange("p (h d) -> p h d", d=HD),
                                      f(vt_hi[:, t, :, 0:HD]), ALU.subtract).then_inc(proj_lo, 1)

                def part_max(b, p):
                    dve.wait_ge(maxmm_done, b * PARTS + p + 1)
                    N = MAXCOLS[p % 2][1]
                    k = 2 * (p % 2)
                    dve.tensor_reduce(mpart[:, p // 2, p % 2:p % 2 + 1], psc[0:HALF, k:k + 2, 0:N], AX.XY, ALU.max).then_inc(max_done, 1)

                def row_max(b):
                    dve.wait_ge(max_done, b * PARTS + PARTS)
                    dve.tensor_tensor(mrow[:], mpart[:, :, 0], mpart[:, :, 1], ALU.max).then_inc(mrow_done, 1)
                    dve.wait_ge(mrow_done, b + 1)
                    for i in range(2):
                        shape = [HALF, KV, HALF]
                        dve.tensor_tensor(mdiag[:, i, :].rearrange("p (a b) -> p a b", a=KV),
                                          negident[:].unsqueeze(1).broadcast_to(shape),
                                          mrow[:, i * KV:(i + 1) * KV].unsqueeze(2).broadcast_to(shape),
                                          ALU.mult).then_inc(mdiag_done, 1)

                def probs_lo(b, u):
                    j = u % UNITS
                    R, N = (VT, 2 * GQ) if j < UNITS - 1 else (Q, GQ)
                    dve.wait_ge(p_hi, b * NU + u + 1)
                    dve.tensor_tensor(prs[1][0:R, u % PRING, 0:N], pr[0:R, u % 2, 0:N], f(prs[0][0:R, u % PRING, 0:N]),
                                      ALU.subtract).then_inc(p_lo, 1)

                def invert(b, h):
                    dve.wait_ge(pv_done, b * NU + (h + 1) * UNITS)
                    dve.wait_ge(stored[h % 2], b * 64 + 32 * (h // 2))
                    dve.reciprocal(osb[HD:HD + 1, h % 2, :], pav[HD:HD + 1, h % 2, 0:GQ]).then_inc(z_done, 1)

                with dve.Fori(0, B) as b:
                    for c in range(CHUNKS):
                        for i in range(KTILES):
                            keys(b, c, i)
                    for t in range(NVT):
                        values(b, t)
                        for p in (2 * t, 2 * t + 1):
                            if p < PARTS:
                                part_max(b, p)
                        if 2 * t + 2 == PARTS:
                            row_max(b)
                    for u in range(NU):
                        probs_lo(b, u)
                        if u >= 9 and (u - 9) % UNITS == AHEAD - 2:
                            invert(b, (u - 9) // UNITS)
                    invert(b, KV - 1)

            @block.tensor
            def _(pe):
                TERMS = ((0, 0), (0, 1), (1, 0))
                pe.wait_ge(consts, 4)

                def project_keys(b, c, i):
                    n = c * KTILES + i
                    if i == 0:
                        pe.wait_ge(ctx_lo, b * LOADS + (c + 1) * HALVES_C)
                    pe.wait_ge(proj_lo, b * NPROJ + max(n - 1, 0))
                    for j in range(3 * KT):
                        a, v = TERMS[j % 3]
                        mm = pe.matmul(pproj[n % 2][:, 0:CS], w["wk"][a][:, j // 3, i * P:(i + 1) * P], ct[v][:, c, j // 3, :],
                                       start=(j == 0), stop=(j == 3 * KT - 1))
                    mm.then_inc(proj_done, 1)

                def project_values(b, t):
                    n = CHUNKS * KTILES + t
                    pe.wait_ge(proj_lo, b * NPROJ + n - 1)
                    s = slice(t % VTC * VT, (t % VTC + 1) * VT)
                    for j in range(3 * KT):
                        a, v = TERMS[j % 3]
                        mm = pe.matmul(pproj[n % 2][0:VT, 0:KD], ct[a][:, t // VTC, j // 3, s], w["wv"][v][:, j // 3, :],
                                       start=(j == 0), stop=(j == 3 * KT - 1))
                    mm.then_inc(proj_done, 1)

                def max_scores(b, p):
                    if p == 0:
                        pe.wait_ge(qk_loaded, b * 160 + 160)
                        pe.wait_ge(exp_done, b * NU)
                    pe.wait_ge(max_done, b * PARTS + max(p - 1, 0))
                    h = p // 2
                    first, N = MAXCOLS[p % 2]
                    for i in range(2):
                        mm = pe.matmul(psc[0:HALF, 2 * (p % 2) + i, 0:N], q[0][0:HD, h * HALF:(h + 1) * HALF],
                                       kt[0][:, h // 2, first + i * N:first + (i + 1) * N], start=True, stop=True)
                    mm.then_inc(maxmm_done, 1)

                def spread_max(b):
                    pe.wait_ge(mdiag_done, 2 * b + 2)
                    pe.wait_ge(o_copied, b * KV)
                    pe.wait_ge(z_done, b * KV)
                    for i in range(2):
                        mm = pe.matmul(pav[:, i, 0:KV * HALF], ones[:], mdiag[:, i, :], start=True, stop=True)
                    mm.then_inc(mb_done, 1)

                def scores(b, u):
                    h, j = u // UNITS, u % UNITS
                    if u < SBANKS:
                        pe.wait_ge(max_done, b * PARTS + PARTS)
                    else:
                        pe.wait_ge(exp_done, b * NU + u - SBANKS + 1)
                    if u == 0:
                        pe.wait_ge(mneg_done, b + 1)
                    tiles = (2 * j, 2 * j + 1) if j < UNITS - 1 else (NVT,)
                    for n, t in enumerate(tiles):
                        s = slice(t * VT, min((t + 1) * VT, SL))
                        R = s.stop - s.start
                        o = psc[0:R, u % SBANKS, n * GQ:(n + 1) * GQ]
                        c = slice(h * GQ, (h + 1) * GQ)
                        pe.matmul(o, kt[1][:, h, s], q[0][:, c], start=True, stop=False)
                        pe.matmul(o, kt[0][:, h, s], q[1][:, c], start=False, stop=False)
                        mm = pe.matmul(o, kt[0][:, h, s], q[0][0:HD, c], start=False, stop=True)
                    mm.then_inc(scores_done, 1)

                def weigh(b, u):
                    h, j = u // UNITS, u % UNITS
                    pe.wait_ge(p_lo, b * NU + u + 1)
                    if u == 0:
                        pe.wait_ge(v_loaded, b * 32 + 32)
                        pe.wait_ge(proj_lo, b * NPROJ + NPROJ)
                    if j == 0 and h >= 2:
                        pe.wait_ge(o_copied, b * KV + h - 1)
                        pe.wait_ge(z_done, b * KV + h - 1)
                    tiles = (2 * j, 2 * j + 1) if j < UNITS - 1 else (NVT,)
                    for n, t in enumerate(tiles):
                        R = VT if t < NVT else Q
                        c = slice(n * GQ, (n + 1) * GQ)
                        o = pav[0:HD + 1, h % 2, 0:GQ]
                        hi, lo = (x[0:R, u % PRING, c] for x in prs)
                        pe.matmul(o, vt_hi[0:R, t, h], hi, start=(t == 0), stop=False)
                        pe.matmul(pav[0:HD, h % 2, 0:GQ], vt_lo[0:R, t, h], hi, start=False, stop=False)
                        mm = pe.matmul(o, vt_hi[0:R, t, h], lo, start=False, stop=(t == NVT))
                    mm.then_inc(pv_done, 1)

                with pe.Fori(0, B) as b:
                    for c in range(CHUNKS):
                        for i in range(KTILES):
                            project_keys(b, c, i)
                    for t in range(NVT):
                        project_values(b, t)
                        for p in (2 * t, 2 * t + 1):
                            if p < PARTS:
                                max_scores(b, p)
                        if t == NVT - 2:
                            spread_max(b)
                    for u in range(AHEAD):
                        scores(b, u)
                    for u in range(NU):
                        if u + AHEAD < NU:
                            scores(b, u + AHEAD)
                        weigh(b, u)


def combine(nc, io, scratch):
    with ExitStack() as ctx:
        sb = lambda name, shape, dt=F32: ctx.enter_context(nc.sbuf_tensor(name, shape, dt))
        sem = lambda name: ctx.enter_context(nc.semaphore(name))
        wo_raw = sb("wo_raw", [P, HT, D])
        wo = [sb(f"wo_{n}", [P, HT, D], F32R) for n in ("hi", "lo")]
        wg = sb("w_gate", [P, KT, E])
        bg = sb("b_gate", [1, E])
        ones = sb("ones_g", [1, P])
        ident = sb("ident_g", [P, P])
        iota_u = sb("iota_u", [P, E], mybir.dt.int32)
        iota = sb("iota_f", [P, E])
        eps = sb("eps_g", [P, 1])
        att = sb("att", [P, 2, HT, P])
        rz = sb("inv_sums", [P, 2, HT, P])
        an = sb("att_scaled", [P, HT, P])
        ats = [sb(f"att_{n}", [P, HT, P], F32R) for n in ("hi", "lo")]
        x = sb("x_rows", [P, 2, D])
        x1 = sb("x1", [P, 2, D + E])
        stats, mv, std, rstd = sb("stats_g", [P, 6]), sb("mv_g", [P, 2]), sb("std_g", [P, 1]), sb("rstd_g", [P, 1])
        xn = sb("xn_g", [P, D])
        xt = sb("xt_g", [P, 2, KT, P])
        lg = sb("logits", [P, E])
        top, topi = sb("top", [P, E]), sb("top_index", [P, E], U32)
        topf = sb("top_index_f", [P, E])
        sel = sb("selected", [P, E])
        po = [ctx.enter_context(nc.psum_tensor(f"ps_o{i}", [P, D], F32)) for i in range(2)]
        pt = ctx.enter_context(nc.psum_tensor("ps_t", [P, KT, P], F32))
        pg = ctx.enter_context(nc.psum_tensor("ps_g", [P, E], F32))

        loaded = [sem(f"rows_loaded{i}") for i in range(2)]
        w_loaded, small_loaded, consts = sem("wo_loaded"), sem("small_loaded"), sem("consts_g")
        w_hi, w_lo = sem("wo_hi_ready"), sem("wo_lo_ready")
        scaled, a_hi, a_lo = sem("att_scaled_done"), sem("att_hi_ready"), sem("att_lo_ready")
        o_done, x1_done = sem("o_done"), sem("x1_done")
        waited = sem("waited_g")
        chain, std_done, normed = sem("dve_chain"), sem("std_done_g"), sem("normed_g")
        turned, xt_done, g_done, gate_done = sem("turned_g"), sem("xt_ready"), sem("gate_logits"), sem("gate_done")
        stored = [sem(f"rows_stored{i}") for i in range(2)]
        att_v = scratch["att"].rearrange("(k p) r -> p k r", p=P)
        x_v = io["x"].rearrange("(t r) d -> t r d", r=P)
        CHAIN = 9
        ROW_LOADS = 16 * (2 + len(HEAD_PIECES))

        with nc.Block() as block:
            @block.sync
            def _(sp):
                def load(t, s):
                    cols = bass.ds(t * P, P)
                    sp.dma_start(att[:, s], att_v[:, :, cols]).then_inc(loaded[s], 16)
                    sp.dma_start(x[:, s], x_v[t]).then_inc(loaded[s], 16)
                    for k, p0, n, h in HEAD_PIECES:
                        src = scratch["rz"][:, cols].rearrange("(a h) r -> h a r", h=4)[h:h + 1]
                        sp.dma_start(rz[p0:p0 + n, s].rearrange("p (a k) r -> p a k r", k=3)[:, :, k, :],
                                     src.broadcast_to([n, HT // 3, P])).then_inc(loaded[s], 16)

                def store(t, s):
                    sp.wait_ge(gate_done, t + 1)
                    sp.dma_start(scratch["x1"][t], x1[:, s]).then_inc(stored[s], 16)
                    sp.wait_ge(xt_done, t + 1)
                    sp.dma_start(scratch["xt"][t], xt[:, s]).then_inc(stored[s], 16)

                load(0, 0)
                sp.dma_start(wo_raw[:], io["wo"]).then_inc(w_loaded, 16)
                sp.dma_start(wg[:], io["wg"]).then_inc(small_loaded, 16)
                sp.dma_start(bg[:], io["bg"]).then_inc(small_loaded, 16)
                load(1, 1)

                def tile(t, s, more):
                    if more:
                        sp.wait_ge(x1_done, t + 1)
                        load(t + 2, s)
                    store(t, s)

                with sp.Fori(0, OT // 2 - 1) as i:
                    for s in range(2):
                        tile(2 * i + s, s, True)
                for s in range(2):
                    tile(OT - 2 + s, s, False)
                for s in range(2):
                    sp.wait_ge(stored[s], 32 * OT // 2)

            @block.gpsimd
            def _(pool):
                pool.memset(eps[:], EPS).then_inc(consts, 1)
                pool.memset(ones[:], 1.0).then_inc(consts, 1)
                pool.memset(ident[:], 0.0).then_inc(consts, 1)
                pool.iota(iota_u[:], pattern=[[1, E]], base=0, channel_multiplier=0).then_inc(consts, 1)
                pool.wait_ge(consts, 4)
                pool.affine_select(out=ident[:], in_=ident[:], compare_op=ALU.not_equal, fill=1.0, base=0,
                                   pattern=[[-1, P]], channel_multiplier=1).then_inc(consts, 1)
                pool.tensor_copy(iota[:], iota_u[:]).then_inc(consts, 1)

            @block.scalar
            def _(act):
                act.wait_ge(consts, 6)
                act.wait_ge(w_loaded, 16)
                for k in range(3):
                    third = slice(k * HT // 3, (k + 1) * HT // 3)
                    act.copy(wo[0][:, third], wo_raw[:, third]).then_inc(w_hi, 1)

                def split(t):
                    act.wait_ge(scaled, t + 1)
                    act.wait_ge(o_done, t)
                    act.copy(ats[0][:], an[:]).then_inc(a_hi, 1)

                def spread(t):
                    act.wait_ge(chain, t * CHAIN + 2)
                    act.activation(std[:], mv[:, 1:2], ACT.Sqrt, bias=eps[:]).then_inc(std_done, 1)

                with act.Fori(0, OT // 2) as i:
                    for s in range(2):
                        t = 2 * i + s
                        split(t)
                        spread(t)
                        act.wait_ge(turned, t + 1)
                        act.wait_ge(stored[s], 32 * i)
                        act.copy(xt[:, s], pt[:]).then_inc(xt_done, 1)

            @block.vector
            def _(dve):
                dve.wait_ge(consts, 6)
                for k in range(3):
                    dve.wait_ge(w_hi, k + 1)
                    third = slice(k * HT // 3, (k + 1) * HT // 3)
                    dve.tensor_tensor(wo[1][:, third], wo_raw[:, third], f(wo[0][:, third]), ALU.subtract).then_inc(w_lo, 1)

                def scale(t, i, s):
                    dve.wait_ge(loaded[s], i * ROW_LOADS + ROW_LOADS)
                    dve.wait_ge(a_lo, t)
                    dve.tensor_tensor(an[:], att[:, s], rz[:, s], ALU.mult).then_inc(scaled, 1)

                with dve.Fori(0, OT // 2) as i:
                    for s in range(2):
                        t = 2 * i + s
                        at = lambda k: t * CHAIN + k
                        scale(t, i, s)
                        dve.wait_ge(a_hi, t + 1)
                        dve.tensor_tensor(ats[1][:], an[:], f(ats[0][:]), ALU.subtract).then_inc(a_lo, 1)
                        dve.wait_ge(o_done, t + 1)
                        dve.wait_ge(stored[s], 32 * i)
                        dve.tensor_tensor(x1[:, s, 0:D], po[s][:], x[:, s], ALU.add).then_inc(x1_done, 1)
                        dve.wait_ge(x1_done, t + 1)
                        dve.bn_stats(stats[:], x1[:, s, 0:D]).then_inc(chain, 1)
                        wait_apart(dve, chain, at(1), waited)
                        dve.bn_aggr(mv[:], stats[:]).then_inc(chain, 1)
                        dve.wait_ge(std_done, t + 1)
                        dve.reciprocal(rstd[:], std[:]).then_inc(chain, 1)
                        dve.wait_ge(chain, at(3))
                        dve.wait_ge(turned, t)
                        dve.tensor_scalar(xn[:], x1[:, s, 0:D], mv[:, 0:1], rstd[:], ALU.subtract, ALU.mult).then_inc(normed, 1)
                        dve.wait_ge(g_done, t + 1)
                        dve.tensor_copy(lg[:], pg[:]).then_inc(chain, 1)
                        wait_apart(dve, chain, at(4), waited)
                        dve.max(top[:], lg[:]).then_inc(chain, 1)
                        wait_apart(dve, chain, at(5), waited)
                        dve.max_index(topi[:], top[:], lg[:]).then_inc(chain, 1)
                        dve.wait_ge(chain, at(6))
                        dve.tensor_copy(topf[:], topi[:]).then_inc(chain, 1)
                        dve.wait_ge(chain, at(7))
                        dve.tensor_scalar(sel[:], iota[:], topf[:, 0:1], 0.5, ALU.is_equal, ALU.mult).then_inc(chain, 1)
                        dve.tensor_scalar(lg[:], iota[:], topf[:, 1:2], 0.5, ALU.is_equal, ALU.mult).then_inc(chain, 1)
                        dve.wait_ge(chain, at(9))
                        dve.tensor_tensor(x1[:, s, D:D + E], sel[:], lg[:], ALU.add).then_inc(gate_done, 1)

            @block.tensor
            def _(pe):
                pe.wait_ge(consts, 6)
                pe.wait_ge(small_loaded, 32)
                with pe.Fori(0, OT // 2) as i:
                    for s in range(2):
                        t = 2 * i + s
                        pe.wait_ge(a_lo, t + 1)
                        pe.wait_ge(w_lo, 3)
                        n = 3 * HT
                        for j in range(n):
                            a, v = ((0, 0), (0, 1), (1, 0))[j % 3]
                            mm = pe.matmul(po[s][:], ats[a][:, j // 3, :], wo[v][:, j // 3, :], start=(j == 0), stop=(j == n - 1))
                        mm.then_inc(o_done, 1)
                        pe.wait_ge(normed, t + 1)
                        for k in range(KT):
                            mm = pe.transpose(pt[:, k, :], xn[:, k * P:(k + 1) * P], ident[:])
                        mm.then_inc(turned, 1)
                        pe.wait_ge(xt_done, t + 1)
                        for k in range(KT):
                            pe.matmul(pg[:], xt[:, s, k, :], wg[:, k, :], start=(k == 0), stop=False)
                        pe.matmul(pg[:], ones[:], bg[:], start=False, stop=True).then_inc(g_done, 1)


def experts(nc, io, scratch, out_d):
    with ExitStack() as ctx:
        sb = lambda name, shape, dt=F32: ctx.enter_context(nc.sbuf_tensor(name, shape, dt))
        sem = lambda name: ctx.enter_context(nc.semaphore(name))
        BANKS, YRING = 4, 2
        we_raw = sb("we_raw", [P, 2, KT, D])
        we = [sb(f"we_{n}", [P, E, KT, D], F32R) for n in ("hi", "lo")]
        be_raw = sb("be_raw", [E, D])
        be_lo = sb("be_lo", [E, D], F32R)
        be = sb("be", [2 * E, D], F32R)
        pick_f = sb("pick_f", [2 * E, E, P])
        pick = sb("pick", [2 * E, E, P], F32R)
        xt = sb("xt_e", [P, 2, KT, P])
        xs = [sb(f"xs_{n}", [P, 2, KT, P], F32R) for n in ("hi", "lo")]
        x1 = sb("x1_e", [P, 2, D + E])
        y = sb("y", [P, YRING, D])
        acc = sb("acc", [P, 2, D])
        po = [ctx.enter_context(nc.psum_tensor(f"ps_e{i}", [P, D], F32)) for i in range(BANKS)]

        w_loaded = [sem(f"we_loaded{i}") for i in range(2)]
        b_loaded, b_moved = sem("be_loaded"), sem("be_moved")
        loaded = [sem(f"tile_loaded{i}") for i in range(2)]
        consts = sem("consts_e")
        w_hi, w_lo, b_hi, b_lo = sem("we_hi_ready"), sem("we_lo_ready"), sem("be_hi_ready"), sem("be_lo_ready")
        x_hi, x_lo = sem("xs_hi_ready"), sem("xs_lo_ready")
        e_done, relu_done, acc_done = sem("expert_done"), sem("relu_done"), sem("acc_done")
        stored = [sem(f"out_stored{i}") for i in range(2)]
        out_v = out_d.rearrange("(t r) d -> t r d", r=P)

        with nc.Block() as block:
            @block.sync
            def _(sp):
                def load(t, s):
                    sp.dma_start(xt[:, s], scratch["xt"][t]).then_inc(loaded[s], 16)
                    sp.dma_start(x1[:, s], scratch["x1"][t]).then_inc(loaded[s], 16)

                load(0, 0)
                sp.dma_start(be_raw[:], io["be"]).then_inc(b_loaded, 16)
                for e in range(E):
                    if e >= 2:
                        sp.wait_ge(w_lo, e - 1)
                    sp.dma_start(we_raw[:, e % 2], io["we"][:, e]).then_inc(w_loaded[e % 2], 16)
                    if e == 1:
                        load(1, 1)
                        sp.wait_ge(b_lo, 1)
                        sp.dma_start(f(be[E:2 * E, :]), f(be_lo[:])).then_inc(b_moved, 16)

                def tile(t, s, more):
                    sp.wait_ge(acc_done, t * E + E)
                    if more:
                        load(t + 2, s)
                    sp.dma_start(out_v[t], acc[:, s]).then_inc(stored[s], 16)

                with sp.Fori(0, OT // 2 - 1) as i:
                    for s in range(2):
                        tile(2 * i + s, s, True)
                for s in range(2):
                    tile(OT - 2 + s, s, False)
                for s in range(2):
                    sp.wait_ge(stored[s], 16 * OT // 2)

            @block.gpsimd
            def _(pool):
                pool.memset(pick_f[:], 0.0).then_inc(consts, 1)
                for n in range(2):
                    pool.wait_ge(consts, n + 1)
                    pool.affine_select(out=pick_f[:], in_=pick_f[:], compare_op=ALU.not_equal, fill=1.0, base=-E * n,
                                       pattern=[[-1, E], [0, P]], channel_multiplier=1).then_inc(consts, 1)

            @block.scalar
            def _(act):
                def split(t, i, s):
                    act.wait_ge(loaded[s], i * 32 + 32)
                    act.copy(xs[0][:, s], xt[:, s]).then_inc(x_hi, 1)

                split(0, 0, 0)
                act.wait_ge(b_loaded, 16)
                act.copy(be[0:E, :], be_raw[:]).then_inc(b_hi, 1)
                for e in range(E):
                    act.wait_ge(w_loaded[e % 2], 16 * (e // 2) + 16)
                    act.copy(we[0][:, e], we_raw[:, e % 2]).then_inc(w_hi, 1)

                def tile(i, s, more):
                    t = 2 * i + s
                    for e in range(E):
                        act.wait_ge(e_done, t * E + e + 1)
                        act.wait_ge(acc_done, t * E + max(e - 1, 0))
                        act.activation(y[:, e % YRING], po[e % BANKS][:], ACT.Relu, scale=x1[:, s, D + e:D + e + 1]).then_inc(relu_done, 1)
                        if e == 2 and more:
                            split(t + 1, i + s, 1 - s)

                with act.Fori(0, OT // 2 - 1) as i:
                    for s in range(2):
                        tile(i, s, True)
                for s in range(2):
                    tile(OT // 2 - 1, s, s == 0)

            @block.vector
            def _(dve):
                def split(t, s):
                    dve.wait_ge(x_hi, t + 1)
                    dve.tensor_tensor(xs[1][:, s], xt[:, s], f(xs[0][:, s]), ALU.subtract).then_inc(x_lo, 1)

                split(0, 0)
                dve.wait_ge(b_hi, 1)
                dve.tensor_tensor(be_lo[:], be_raw[:], f(be[0:E, :]), ALU.subtract).then_inc(b_lo, 1)
                dve.wait_ge(consts, 3)
                dve.tensor_copy(pick[:], pick_f[:]).then_inc(consts, 1)
                for e in range(E):
                    dve.wait_ge(w_hi, e + 1)
                    dve.tensor_tensor(we[1][:, e], we_raw[:, e % 2], f(we[0][:, e]), ALU.subtract).then_inc(w_lo, 1)

                def tile(i, s, more):
                    t = 2 * i + s
                    dve.wait_ge(stored[s], 16 * i)
                    for e in range(E):
                        dve.wait_ge(relu_done, t * E + e + 1)
                        dve.wait_ge(acc_done, t * E + e)
                        dve.tensor_tensor(acc[:, s], x1[:, s, 0:D] if e == 0 else acc[:, s], y[:, e % YRING], ALU.add).then_inc(acc_done, 1)
                        if e == 2 and more:
                            split(t + 1, 1 - s)

                with dve.Fori(0, OT // 2 - 1) as i:
                    for s in range(2):
                        tile(i, s, True)
                for s in range(2):
                    tile(OT // 2 - 1, s, s == 0)

            @block.tensor
            def _(pe):
                pe.wait_ge(consts, 4)
                pe.wait_ge(b_moved, 16)
                with pe.Fori(0, OT // 2) as i:
                    for s in range(2):
                        t = 2 * i + s
                        pe.wait_ge(x_lo, t + 1)
                        for e in range(E):
                            pe.wait_ge(w_lo, e + 1)
                            pe.wait_ge(relu_done, t * E + max(e - BANKS + 1, 0))
                            for j in range(3 * KT):
                                a, v = ((0, 0), (0, 1), (1, 0))[j % 3]
                                pe.matmul(po[e % BANKS][:], xs[a][:, s, j // 3, :], we[v][:, e, j // 3, :], start=(j == 0), stop=False)
                            pe.matmul(po[e % BANKS][:], pick[:, e, :], be[:], start=False, stop=True).then_inc(e_done, 1)


def build(nc, io, out_d):
    scratch = {
        "qk": [nc.dram_tensor(f"qk_{n}", (B, HH + KD, Q), F32, kind="Internal").ap() for n in ("hi", "lo")],
        "v": [nc.dram_tensor(f"v_{n}", (ROWS, KD), F32, kind="Internal").ap() for n in ("hi", "lo")],
        "att": nc.dram_tensor("att_t", (HH, ROWS), F32, kind="Internal").ap(),
        "rz": nc.dram_tensor("rz", (H, ROWS), F32, kind="Internal").ap(),
        "x1": nc.dram_tensor("x1_gate", (OT, P, D + E), F32, kind="Internal").ap(),
        "xt": nc.dram_tensor("xt_normed", (OT, P, KT * P), F32, kind="Internal").ap(),
    }
    scratch["xt"] = scratch["xt"].rearrange("t p (k r) -> t p k r", k=KT)
    with ExitStack() as ctx:
        w = {name: [ctx.enter_context(nc.sbuf_tensor(f"{name}_{n}", [P, KT, KD], F32R)) for n in ("hi", "lo")]
             for name in ("wk", "wv")}
        project(nc, w, io, scratch)
        attend(nc, w, io, scratch)
    combine(nc, io, scratch)
    experts(nc, io, scratch, out_d)


def kernel(x, ctx_4096, L0_xattn_Wq, L0_xattn_Wk, L0_xattn_Wv, L0_xattn_Wo, L0_ffn_W_gate, L0_ffn_b_gate,
           L0_ffn_W_e, L0_ffn_b_e):
    import numpy as np
    import concourse.bacc as bacc
    from concourse.bass_utils import run_bass_kernel_spmd

    def stationary(w):
        return w.T.reshape(-1, P, w.shape[0]).transpose(1, 0, 2)

    wk = np.asarray(L0_xattn_Wk)
    last = wk[KTILES * HD:]
    wk_tiles = np.concatenate([part for i in range(KTILES)
                               for part in (wk[i * HD:(i + 1) * HD], last[i * PIECE:(i + 1) * PIECE])])
    arrays = {
        "x": np.asarray(x).reshape(ROWS, D),
        "ctx": np.asarray(ctx_4096).reshape(B, CHUNKS, CS, KT, P).transpose(0, 1, 4, 3, 2),
        "wq": stationary(np.asarray(L0_xattn_Wq)),
        "wk": stationary(wk_tiles),
        "wv": stationary(np.asarray(L0_xattn_Wv)),
        "wo": stationary(np.asarray(L0_xattn_Wo)),
        "wg": np.asarray(L0_ffn_W_gate).reshape(KT, P, E).transpose(1, 0, 2),
        "bg": np.asarray(L0_ffn_b_gate).reshape(1, E),
        "we": np.asarray(L0_ffn_W_e).reshape(E, KT, P, D).transpose(2, 0, 1, 3),
        "be": np.asarray(L0_ffn_b_e),
    }
    arrays = {k: np.ascontiguousarray(v) for k, v in arrays.items()}
    nc = bacc.Bacc("TRN2", target_bir_lowering=False, num_devices=1)
    io = {k: nc.dram_tensor(f"in_{k}", v.shape, F32, kind="ExternalInput").ap() for k, v in arrays.items()}
    out_d = nc.dram_tensor("out", (ROWS, D), F32, kind="ExternalOutput").ap()
    build(nc, io, out_d)
    r = run_bass_kernel_spmd(nc, [{f"in_{k}": v for k, v in arrays.items()}], core_ids=[0])
    return r.results[0]["out"].reshape(B, Q, D)
```

```python
from contextlib import ExitStack

import concourse.bass as bass
from concourse import mybir

F32 = mybir.dt.float32
F32R = mybir.dt.float32r
U32 = mybir.dt.uint32
ALU = mybir.AluOpType
ACT = mybir.ActivationFunctionType
AX = mybir.AxisListType

P = 128
B, Q, D = 32, 56, 512
S = 1500
H, KV, HD = 16, 4, 96
G = H // KV
E = 8
EPS = 1e-5
SCALE = float(HD) ** -0.5
KT = D // P
ROWS = B * Q
SL = S + Q
GQ = G * Q
KD = KV * HD
HH = H * HD

PIECE = P - HD
KTILES = KD // P
CHUNKS = 3
CS = S // CHUNKS
HALVES_C = 2
KH = KT // HALVES_C
LOADS = CHUNKS * HALVES_C
RAW = 3
VT = 125
VTC = CS // VT
NVT = S // VT

GROUPS = 4
GR = ROWS // GROUPS
RT = 112
GT = GR // RT
MQ = HH // P
MK = MQ + KTILES
NOUT = MK + GT
WQP = HH // KD
OSLOTS, OBANKS = 3, 4

HALVES = 2 * KV
HALF = GQ // 2
MAXCOLS = [(0, 390), (780, 388)]
PARTS = 2 * HALVES
UNITS = 7
NU = KV * UNITS
SBANKS = 4
AHEAD = 3
PRING = 4
NPROJ = CHUNKS * KTILES + NVT
NHI = 2 * CHUNKS * KTILES + NVT

OT = ROWS // P
HT = HH // P
WOT = HT // LOADS
HEAD_PIECES = [(0, 0, 96, 0), (0, 96, 32, 1), (1, 0, 64, 1), (1, 64, 64, 2), (2, 0, 32, 2), (2, 32, 96, 3)]


START = 1
TERMS = ((0, 0), (0, 1), (1, 0))


def wait_apart(eng, sem, value, waited):
    eng.wait_ge(sem, value)
    eng.sem_inc(waited, 1)


def f(ap):
    return ap.bitcast(F32)


def load_ctx(sp, stream, io, b, n, first=False):
    if not (first and n < RAW):
        sp.wait_ge(stream["lo"], b * LOADS + n - RAW + 1)
    k = n % HALVES_C * KH
    sp.dma_start(stream["raw"][:, n % RAW], io["ctx"][b, n // HALVES_C, :, k:k + KH, :]).then_inc(stream["loaded"][n % RAW], 16)


def split(pool, stream, b, n, raw, parts):
    wait_apart(pool, stream["loaded"][n % RAW], b * 32 + n // RAW * 16 + 16, stream["waited"])
    hi, lo = parts
    pool.tensor_scalar(hi, raw, 1.0, 0.0, ALU.mult, ALU.add).then_inc(stream["hi"], 1)
    pool.wait_ge(stream["hi"], b * LOADS + n + 1)
    pool.tensor_tensor(lo, raw, f(hi), ALU.subtract).then_inc(stream["lo"], 1)


def split_ctx(pool, stream, b, n):
    c, k = n // HALVES_C, n % HALVES_C * KH
    split(pool, stream, b, n, stream["raw"][:, n % RAW], [p[:, c, k:k + KH] for p in stream["parts"]])


def load_wo(sp, stream, io, n):
    sp.wait_ge(stream["lo"], B * LOADS + n - RAW + 1)
    raw = stream["raw_full"][:, n % RAW].rearrange("p (t d) -> p t d", d=D)
    sp.dma_start(raw, io["wo"][:, n * WOT:(n + 1) * WOT]).then_inc(stream["loaded"][n % RAW], 16)


def split_wo(pool, stream, n):
    split(pool, stream, B, n, stream["raw_full"][:, n % RAW].rearrange("p (t d) -> p t d", d=D),
          [p[:, n * WOT:(n + 1) * WOT] for p in stream["wo"]])


def project(nc, w, stream, io, scratch):
    with ExitStack() as ctx:
        sb = lambda name, shape, dt=F32: ctx.enter_context(nc.sbuf_tensor(name, shape, dt))
        sem = lambda name: ctx.enter_context(nc.semaphore(name))
        w_raw = sb("w_raw", [P, 2, KT, KD])
        wq = [sb(f"wq_{n}", [P, KT, HH], F32R) for n in ("hi", "lo")]
        x = sb("x_group", [RT, GT, D])
        xn = sb("x_normed", [RT, GT, D])
        stats = sb("ln_stats", [RT, GT, 6])
        mv = sb("ln_mean_var", [RT, GT, 2])
        std = sb("ln_std", [RT, GT])
        rstd = sb("ln_rstd", [RT, GT])
        eps = sb("eps_p", [P, 1])
        ident = sb("ident_p", [P, P])
        xt = [sb(f"xt_{n}", [P, KT, GR], F32R) for n in ("hi", "lo")]
        out = [sb(f"proj_out_{n}", [P, OSLOTS, GR], F32R) for n in ("hi", "lo")]
        pt = [ctx.enter_context(nc.psum_tensor(f"ps_xt{i}", [P, GR], F32)) for i in range(KT)]
        po = [ctx.enter_context(nc.psum_tensor(f"ps_out{i}", [P, GR], F32)) for i in range(OBANKS)]

        waited = sem("waited_p")
        x_loaded = sem("x_loaded")
        w_loaded = [sem(f"w_loaded{i}") for i in range(2)]
        consts = sem("consts_ready")
        stats_done, mv_done, std_done, rstd_done = sem("stats_done"), sem("mv_done"), sem("std_done"), sem("rstd_done")
        normed = sem("normed")
        turned = sem("turned")
        xt_hi, xt_lo = sem("xt_hi_ready"), sem("xt_lo_ready")
        w_hi, w_lo = sem("w_hi_ready"), sem("w_lo_ready")
        out_done = sem("out_done")
        out_hi, out_lo = sem("out_hi_ready"), sem("out_lo_ready")
        stored = [sem(f"stored{i}") for i in range(OSLOTS)]
        xg = io["x"].rearrange("(g t r) d -> g r t d", t=GT, r=RT)
        qk_d = [s.rearrange("m (g c) -> g m c", c=GR) for s in scratch["qk"]]
        v_d = [s.rearrange("(g t r) n -> g t r n", t=GT, r=RT) for s in scratch["v"]]
        cols = lambda i: slice(i * KD, (i + 1) * KD)
        w_from = [io["wq"][:, :, cols(i)] for i in range(WQP)] + [io["wk"], io["wv"]]
        w_to = [[t[:, :, cols(i)] for t in wq] for i in range(WQP)] + [[t[:] for t in w[n]] for n in ("wk", "wv")]

        def uses(i):
            return len(range(i, NOUT, OSLOTS))

        with nc.Block() as block:
            @block.sync
            def _(sp):
                for s in stored:
                    sp.sem_inc(s, START)
                sp.dma_start(x[:], xg[0]).then_inc(x_loaded, 16)

                def load_w(i):
                    if i >= 2:
                        sp.wait_ge(w_lo, i - 1)
                    sp.dma_start(w_raw[:, i % 2], w_from[i]).then_inc(w_loaded[i % 2], 16)

                for i in range(4):
                    load_w(i)

                def group(g, more, first=False):
                    if more:
                        sp.wait_ge(normed, g * GT + GT)
                        sp.dma_start(x[:], xg[g + 1]).then_inc(x_loaded, 16)
                    for n in range(NOUT):
                        if not more and n < 3 * LOADS and n % 3 == 0:
                            load_ctx(sp, stream, io, 0, n // 3, first=True)
                        sp.wait_ge(out_lo, START + g * NOUT + n + 1)
                        for i in range(2):
                            if n < MK:
                                src, dst = f(out[i][:, n % OSLOTS, :]), qk_d[i][g, n * P:(n + 1) * P]
                            else:
                                src, dst = f(out[i][0:RT, n % OSLOTS, 0:KD]), v_d[i][g, n - MK]
                            sp.dma_start(dst, src).then_inc(stored[n % OSLOTS], 16)
                        if first and n in (2, 5):
                            load_w(n // 3 + 4)

                group(0, True, first=True)
                with sp.Fori(1, GROUPS - 1) as g:
                    group(g, True)
                group(GROUPS - 1, False)
                for i in range(OSLOTS):
                    sp.wait_ge(stored[i], START + 32 * GROUPS * uses(i))

            @block.gpsimd
            def _(pool):
                pool.memset(eps[:], EPS).then_inc(consts, 1)
                pool.memset(ident[:], 0.0).then_inc(consts, 1)
                pool.wait_ge(consts, 2)
                pool.affine_select(out=ident[:], in_=ident[:], compare_op=ALU.not_equal, fill=1.0, base=0,
                                   pattern=[[-1, P]], channel_multiplier=1).then_inc(consts, 1)
                for n in range(LOADS):
                    split_ctx(pool, stream, 0, n)

            @block.scalar
            def _(act):
                def norm_scale(g):
                    act.wait_ge(mv_done, g * GT + GT)
                    act.activation(std[:], mv[:, :, 1], ACT.Sqrt, bias=eps[0:RT]).then_inc(std_done, 1)

                def split_out(g, n):
                    act.wait_ge(out_done, START + g * NOUT + n + 1)
                    act.wait_ge(stored[n % OSLOTS], START + g * (32 * uses(n % OSLOTS)) + 32 * (n // OSLOTS))
                    R, N = (P, GR) if n < MK else (RT, KD)
                    act.copy(out[0][0:R, n % OSLOTS, 0:N], po[n % OBANKS][0:R, 0:N]).then_inc(out_hi, 1)

                def turn(g):
                    for k in range(KT):
                        act.wait_ge(turned, START + g * KT + k + 1)
                        if k == 0:
                            act.wait_ge(out_done, START + g * NOUT)
                        act.copy(xt[0][:, k, :], pt[k][:]).then_inc(xt_hi, 1)

                def split_w(i):
                    act.wait_ge(w_loaded[i % 2], 16 * (i // 2) + 16)
                    act.copy(w_to[i][0], w_raw[:, i % 2]).then_inc(w_hi, 1)

                split_w(0)
                act.wait_ge(consts, 3)
                norm_scale(0)
                turn(0)
                split_w(1)

                def group(g, more, first=False):
                    for n in range(NOUT):
                        split_out(g, n)
                        if first and n % KTILES == 1 and n // KTILES + 2 < len(w_to):
                            split_w(n // KTILES + 2)
                        if n == 6 and more:
                            norm_scale(g + 1)
                    if more:
                        turn(g + 1)

                group(0, True, first=True)
                with act.Fori(1, GROUPS - 1) as g:
                    group(g, True)
                group(GROUPS - 1, False)

            @block.vector
            def _(dve):
                for s in (xt_lo, out_lo):
                    dve.sem_inc(s, START)
                def moments(g):
                    dve.wait_ge(x_loaded, g * 16 + 16)
                    for t in range(GT):
                        dve.bn_stats(stats[:, t, :], x[:, t, :]).then_inc(stats_done, 1)
                    for t in range(GT):
                        wait_apart(dve, stats_done, g * GT + t + 1, waited)
                        dve.bn_aggr(mv[:, t, :], stats[:, t, :]).then_inc(mv_done, 1)

                def norm(g):
                    dve.wait_ge(std_done, g + 1)
                    dve.wait_ge(turned, START + g * KT)
                    dve.reciprocal(rstd[:], std[:]).then_inc(rstd_done, 1)
                    dve.wait_ge(rstd_done, g + 1)
                    for t in range(GT):
                        dve.tensor_scalar(xn[:, t, :], x[:, t, :], mv[:, t, 0:1], rstd[:, t:t + 1],
                                          ALU.subtract, ALU.mult).then_inc(normed, 1)

                def split_out(g, n):
                    dve.wait_ge(out_hi, g * NOUT + n + 1)
                    R, N = (P, GR) if n < MK else (RT, KD)
                    dve.tensor_tensor(out[1][0:R, n % OSLOTS, 0:N], po[n % OBANKS][0:R, 0:N],
                                      f(out[0][0:R, n % OSLOTS, 0:N]), ALU.subtract).then_inc(out_lo, 1)

                def turn(g):
                    for k in range(KT):
                        dve.wait_ge(xt_hi, g * KT + k + 1)
                        dve.tensor_tensor(xt[1][:, k, :], pt[k][:], f(xt[0][:, k, :]), ALU.subtract).then_inc(xt_lo, 1)

                def split_w(i):
                    dve.wait_ge(w_hi, i + 1)
                    dve.tensor_tensor(w_to[i][1], w_raw[:, i % 2], f(w_to[i][0]), ALU.subtract).then_inc(w_lo, 1)

                moments(0)
                split_w(0)
                norm(0)
                turn(0)
                split_w(1)

                def group(g, more, first=False):
                    for n in range(NOUT):
                        split_out(g, n)
                        if first and n % KTILES == 1 and n // KTILES + 2 < len(w_to):
                            split_w(n // KTILES + 2)
                        if n == 4 and more:
                            moments(g + 1)
                        if n == 8 and more:
                            norm(g + 1)
                    if more:
                        turn(g + 1)

                group(0, True, first=True)
                with dve.Fori(1, GROUPS - 1) as g:
                    group(g, True)
                group(GROUPS - 1, False)

            @block.tensor
            def _(pe):
                for s in (turned, out_done):
                    pe.sem_inc(s, START)
                pe.wait_ge(consts, 3)

                def turn(g):
                    pe.wait_ge(normed, g * GT + GT)
                    pe.wait_ge(xt_lo, START + g * KT)
                    for k in range(KT):
                        for t in range(GT):
                            mm = pe.transpose(pt[k][:, t * RT:(t + 1) * RT], xn[:, t, k * P:(k + 1) * P], ident[0:RT, 0:RT])
                        mm.then_inc(turned, 1)

                def product(g, n):
                    pe.wait_ge(out_lo, START + g * NOUT + max(n - OBANKS + 1, 0))
                    last = 3 * KT - 1
                    for j in range(3 * KT):
                        k, (a, b) = j // 3, TERMS[j % 3]
                        if n == 0 and j % 3 == 0:
                            pe.wait_ge(xt_lo, START + g * KT + k + 1)
                        if n < MK:
                            stat = wq[a][:, k, n * P:(n + 1) * P] if n < MQ else w["wk"][a][:, k, (n - MQ) * P:(n - MQ + 1) * P]
                            mm = pe.matmul(po[n % OBANKS][:, :], stat, xt[b][:, k, :], start=(j == 0), stop=(j == last))
                        else:
                            t = n - MK
                            mm = pe.matmul(po[n % OBANKS][0:RT, 0:KD], xt[a][:, k, t * RT:(t + 1) * RT], w["wv"][b][:, k, :],
                                           start=(j == 0), stop=(j == last))
                    mm.then_inc(out_done, 1)

                def group(g, more):
                    for n in range(NOUT):
                        if n % KTILES == 0 and n <= MK:
                            pe.wait_ge(w_lo, n // KTILES + 1)
                        product(g, n)
                        if n == NOUT - 4 and more:
                            turn(g + 1)

                turn(0)
                with pe.Fori(0, GROUPS - 1) as g:
                    group(g, True)
                group(GROUPS - 1, False)


def attend(nc, w, stream, io, scratch):
    with ExitStack() as ctx:
        sb = lambda name, shape, dt=F32: ctx.enter_context(nc.sbuf_tensor(name, shape, dt))
        sem = lambda name: ctx.enter_context(nc.semaphore(name))
        ct = stream["parts"]
        kt = [sb("keys_hi", [HD, KV, SL], F32R), sb("keys_lo", [HD + 1, KV, SL], F32R)]
        vt_hi = sb("values_hi", [VT, NVT + 1, KV, HD + 1], F32R)
        vt_lo = sb("values_lo", [VT, NVT + 1, KV, HD], F32R)
        q = [sb("queries_hi", [HD + 1, KV * GQ], F32R), sb("queries_lo", [HD, KV * GQ], F32R)]
        pr = sb("probs", [VT, PRING, 2 * GQ])
        prs = [sb(f"probs_{n}", [VT, PRING, 2 * GQ], F32R) for n in ("hi", "lo")]
        mpart = sb("max_parts", [HALF, HALVES, 2])
        mrow = sb("max_rows", [HALF, HALVES])
        mdiag = prs[1][0:HALF, 0:2, 0:KV * HALF]
        negident = sb("neg_ident", [HALF, HALF])
        ones = sb("ones_a", [HALF, P], F32R)
        osb = sb("attended", [HD + 1, 2, GQ])
        pproj = [ctx.enter_context(nc.psum_tensor(f"ps_proj{i}", [P, 512], F32)) for i in range(2)]
        psc = ctx.enter_context(nc.psum_tensor("ps_scores", [P, SBANKS, 512], F32))
        pav = ctx.enter_context(nc.psum_tensor("ps_attended", [P, 2, 512], F32))

        ctx_lo = stream["lo"]
        qk_loaded, v_loaded = sem("qk_loaded"), sem("v_loaded")
        cleared = sem("ident_cleared")
        consts = sem("consts_ready_a")
        proj_done = sem("proj_done")
        proj_hi, proj_lo = sem("proj_hi_ready"), sem("proj_lo_ready")
        maxmm_done, max_done = sem("max_scores_done"), sem("max_done")
        mrow_done, mdiag_done, mb_done, mneg_done = sem("max_rows_done"), sem("max_diag_done"), sem("max_spread"), sem("max_in_queries")
        scores_done, exp_done, p_hi, p_lo = sem("scores_done"), sem("exp_done"), sem("p_hi_ready"), sem("p_lo_ready")
        pv_done = sem("pv_done")
        o_copied, z_inverted = sem("o_copied"), sem("sums_inverted")
        stored = [sem(f"att_stored{i}") for i in range(2)]

        q_d = [s[0:HH].rearrange("(h d) (b q) -> b d h q", d=HD, q=Q) for s in scratch["qk"]]
        k_d = [s[HH:HH + KD].rearrange("(i r) (b q) -> b i r q", r=P, q=Q) for s in scratch["qk"]]
        att_d = scratch["att"].rearrange("(h d) (b q) -> b d h q", d=HD, q=Q)
        rz_d = scratch["rz"].rearrange("h (b q) -> b h q", q=Q)

        with nc.Block() as block:
            @block.sync
            def _(sp):
                for s in stored:
                    sp.sem_inc(s, START)
                def load_qk(b):
                    for i in range(2):
                        sp.dma_start(f(q[i][0:HD, :]).rearrange("d (h q) -> d h q", q=Q), q_d[i][b]).then_inc(qk_loaded, 16)
                        rows = k_d[i][b]
                        sp.dma_start(f(kt[i][0:HD, 0:KTILES, S:SL]),
                                     rows[:, 0:HD].rearrange("i r q -> r i q")).then_inc(qk_loaded, 16)
                        for j in range(KTILES):
                            sp.dma_start(f(kt[i][j * PIECE:(j + 1) * PIECE, KTILES, S:SL]),
                                         rows[j, HD:P]).then_inc(qk_loaded, 16)

                def load_v(b):
                    for i, dst in enumerate((vt_hi[0:Q, NVT, :, 0:HD], vt_lo[0:Q, NVT])):
                        sp.dma_start(f(dst), scratch["v"][i].rearrange("(b q) (h d) -> b q h d", q=Q, d=HD)[b]).then_inc(v_loaded, 16)

                def store_sums(b, h):
                    sp.wait_ge(z_inverted, START + b * H + (h + 1) * G)
                    sp.dma_start(rz_d[bass.ds(b, 1), h * G:(h + 1) * G, :],
                                 osb[HD:HD + 1, h % 2, :].rearrange("d (h q) -> d h q", q=Q)).then_inc(stored[h % 2], 16)

                def store(b):
                    for h in range(KV):
                        sp.wait_ge(o_copied, START + b * KV + h + 1)
                        sp.dma_start(att_d[b, :, h * G:(h + 1) * G, :],
                                     osb[0:HD, h % 2, :].rearrange("d (h q) -> d h q", q=Q)).then_inc(stored[h % 2], 16)
                        if h < KV - 1:
                            store_sums(b, h)

                load_qk(0)
                load_v(0)
                with sp.Fori(0, B - 1) as b:
                    for n in range(LOADS):
                        load_ctx(sp, stream, io, b + 1, n)
                    store(b)
                    sp.wait_ge(scores_done, b * NU + NU)
                    load_qk(b + 1)
                    sp.wait_ge(pv_done, START + b * NU + NU)
                    load_v(b + 1)
                    store_sums(b, KV - 1)
                for n in range(LOADS):
                    load_wo(sp, stream, io, n)
                store(B - 1)
                store_sums(B - 1, KV - 1)
                for i in range(2):
                    sp.wait_ge(stored[i], START + B * KV // 2 * 32)

            @block.gpsimd
            def _(pool):
                pool.memset(negident[:], 0.0).then_inc(cleared, 1)
                pool.wait_ge(cleared, 1)
                pool.affine_select(out=negident[:], in_=negident[:], compare_op=ALU.not_equal, fill=-1.0, base=0,
                                   pattern=[[-1, HALF]], channel_multiplier=1).then_inc(consts, 1)
                for n, ap in enumerate((ones[:], kt[1][HD:HD + 1], vt_hi[:, :, :, HD:HD + 1])):
                    pool.wait_ge(consts, n + 1)
                    pool.memset(f(ap), 1.0).then_inc(consts, 1)

                with pool.Fori(1, B) as b:
                    for n in range(LOADS):
                        if n % HALVES_C == 0:
                            pool.wait_ge(proj_done, (b - 1) * NPROJ + CHUNKS * KTILES + (n // HALVES_C + 1) * VTC)
                        split_ctx(pool, stream, b, n)
                pool.wait_ge(proj_done, B * NPROJ)
                for n in range(LOADS):
                    split_wo(pool, stream, n)

            @block.scalar
            def _(act):
                for s in (exp_done, o_copied):
                    act.sem_inc(s, START)
                def keys(b, c, i):
                    s = slice(c * CS, (c + 1) * CS)
                    n = c * KTILES + i
                    act.wait_ge(proj_done, b * NPROJ + n + 1)
                    act.copy(kt[0][0:HD, i, s], pproj[n % 2][0:HD, 0:CS]).then_inc(proj_hi, 1)
                    act.copy(kt[0][i * PIECE:(i + 1) * PIECE, KTILES, s], pproj[n % 2][HD:P, 0:CS]).then_inc(proj_hi, 1)

                def values(b, t):
                    n = CHUNKS * KTILES + t
                    act.wait_ge(proj_done, b * NPROJ + n + 1)
                    act.copy(vt_hi[:, t, :, 0:HD], pproj[n % 2][0:VT, 0:KD].rearrange("p (h d) -> p h d", d=HD)).then_inc(proj_hi, 1)

                def exp(b, u):
                    j = u % UNITS
                    R, N = (VT, 2 * GQ) if j < UNITS - 1 else (Q, GQ)
                    act.wait_ge(scores_done, b * NU + u + 1)
                    act.wait_ge(p_lo, START + b * NU + max(u - PRING + 1, 0))
                    act.activation(pr[0:R, u % PRING, 0:N], psc[0:R, u % SBANKS, 0:N], ACT.Exp, scale=SCALE).then_inc(exp_done, 1)

                def probs_hi(b, u):
                    j = u % UNITS
                    R, N = (VT, 2 * GQ) if j < UNITS - 1 else (Q, GQ)
                    act.wait_ge(exp_done, START + b * NU + u + 1)
                    act.wait_ge(pv_done, START + b * NU + max(u - PRING + 1, 0))
                    act.copy(prs[0][0:R, u % PRING, 0:N], pr[0:R, u % PRING, 0:N]).then_inc(p_hi, 1)

                def take_out(b, h):
                    act.wait_ge(pv_done, START + b * NU + (h + 1) * UNITS)
                    act.wait_ge(stored[h % 2], START + b * 64 + 32 * (h // 2))
                    act.copy(osb[0:HD, h % 2, :], pav[0:HD, h % 2, 0:GQ]).then_inc(o_copied, 1)

                with act.Fori(0, B) as b:
                    for c in range(CHUNKS):
                        for i in range(KTILES):
                            keys(b, c, i)
                    for t in range(NVT):
                        values(b, t)
                        if t == NVT - 2:
                            exp(b, 0)
                            probs_hi(b, 0)
                            exp(b, 1)
                        if t == NVT - 3:
                            act.wait_ge(mb_done, b + 1)
                            act.copy(q[0][HD:HD + 1, :], pav[HD:HD + 1, :, 0:KV * HALF]).then_inc(mneg_done, 1)
                    probs_hi(b, 1)
                    for u in range(2, NU):
                        exp(b, u)
                        probs_hi(b, u)
                        if u > UNITS and u % UNITS == AHEAD - 1:
                            take_out(b, u // UNITS - 1)
                    take_out(b, KV - 1)


            @block.vector
            def _(dve):
                for s in (p_lo, proj_lo, max_done, z_inverted):
                    dve.sem_inc(s, START)
                def keys(b, c, i):
                    s = slice(c * CS, (c + 1) * CS)
                    n = c * KTILES + i
                    dve.wait_ge(proj_hi, b * NHI + 2 * n + 1)
                    dve.tensor_tensor(kt[1][0:HD, i, s], pproj[n % 2][0:HD, 0:CS], f(kt[0][0:HD, i, s]), ALU.subtract)
                    piece = slice(i * PIECE, (i + 1) * PIECE)
                    dve.wait_ge(proj_hi, b * NHI + 2 * n + 2)
                    dve.tensor_tensor(kt[1][piece, KTILES, s], pproj[n % 2][HD:P, 0:CS], f(kt[0][piece, KTILES, s]),
                                      ALU.subtract).then_inc(proj_lo, 1)

                def values(b, t):
                    n = CHUNKS * KTILES + t
                    dve.wait_ge(proj_hi, b * NHI + NHI - NVT + t + 1)
                    dve.tensor_tensor(vt_lo[:, t], pproj[n % 2][0:VT, 0:KD].rearrange("p (h d) -> p h d", d=HD),
                                      f(vt_hi[:, t, :, 0:HD]), ALU.subtract).then_inc(proj_lo, 1)

                def part_max(b, p):
                    dve.wait_ge(maxmm_done, b * PARTS + p + 1)
                    N = MAXCOLS[p % 2][1]
                    k = 2 * (p % 2)
                    dve.tensor_reduce(mpart[:, p // 2, p % 2:p % 2 + 1], psc[0:HALF, k:k + 2, 0:N], AX.XY, ALU.max).then_inc(max_done, 1)

                def row_max(b):
                    dve.wait_ge(consts, 4)
                    dve.wait_ge(max_done, START + b * PARTS + PARTS)
                    dve.tensor_tensor(mrow[:], mpart[:, :, 0], mpart[:, :, 1], ALU.max).then_inc(mrow_done, 1)
                    dve.wait_ge(mrow_done, b + 1)
                    for i in range(2):
                        shape = [HALF, KV, HALF]
                        dve.tensor_tensor(mdiag[:, i, :].rearrange("p (a b) -> p a b", a=KV),
                                          negident[:].unsqueeze(1).broadcast_to(shape),
                                          mrow[:, i * KV:(i + 1) * KV].unsqueeze(2).broadcast_to(shape),
                                          ALU.mult).then_inc(mdiag_done, 1)

                def probs_lo(b, u):
                    j = u % UNITS
                    R, N = (VT, 2 * GQ) if j < UNITS - 1 else (Q, GQ)
                    dve.wait_ge(p_hi, b * NU + u + 1)
                    dve.tensor_tensor(prs[1][0:R, u % PRING, 0:N], pr[0:R, u % PRING, 0:N], f(prs[0][0:R, u % PRING, 0:N]),
                                      ALU.subtract).then_inc(p_lo, 1)

                def invert_sums(b, h, g):
                    dve.wait_ge(pv_done, START + b * NU + (h + 1) * UNITS)
                    dve.wait_ge(stored[h % 2], START + b * 64 + 32 * (h // 2))
                    s = slice(g * Q, (g + 1) * Q)
                    dve.reciprocal(osb[HD:HD + 1, h % 2, s], pav[HD:HD + 1, h % 2, s]).then_inc(z_inverted, 1)

                def batch(b, first=False):
                    for c in range(CHUNKS):
                        for i in range(KTILES):
                            keys(b, c, i)
                            n = c * KTILES + i
                            if not first and 2 <= n < 2 + G:
                                invert_sums(b - 1, KV - 1, n - 2)
                    for t in range(NVT):
                        if 2 * t < PARTS:
                            part_max(b, 2 * t)
                        values(b, t)
                        if 2 * t < PARTS:
                            part_max(b, 2 * t + 1)
                        if 2 * t + 2 == PARTS:
                            row_max(b)
                        if t == NVT - 2:
                            probs_lo(b, 0)
                    for u in range(1, NU):
                        probs_lo(b, u)
                        if u > UNITS and 1 <= u % UNITS < 1 + G:
                            invert_sums(b, u // UNITS - 1, u % UNITS - 1)

                batch(0, first=True)
                with dve.Fori(1, B) as b:
                    batch(b)
                for g in range(G):
                    invert_sums(B - 1, KV - 1, g)

            @block.tensor
            def _(pe):
                pe.sem_inc(pv_done, START)
                def project_keys(b, c, i):
                    n = c * KTILES + i
                    if i == 0:
                        pe.wait_ge(ctx_lo, b * LOADS + (c + 1) * HALVES_C)
                    pe.wait_ge(proj_lo, START + b * NPROJ + max(n - 1, 0))
                    for j in range(3 * KT):
                        a, v = TERMS[j % 3]
                        mm = pe.matmul(pproj[n % 2][:, 0:CS], w["wk"][a][:, j // 3, i * P:(i + 1) * P], ct[v][:, c, j // 3, :],
                                       start=(j == 0), stop=(j == 3 * KT - 1))
                    mm.then_inc(proj_done, 1)

                def project_values(b, t, part):
                    n = CHUNKS * KTILES + t
                    if part == 0:
                        pe.wait_ge(proj_lo, START + b * NPROJ + n - 1)
                    s = slice(t % VTC * VT, (t % VTC + 1) * VT)
                    half = 3 * KT // 2
                    for j in range(part * half, part * half + half):
                        a, v = TERMS[j % 3]
                        mm = pe.matmul(pproj[n % 2][0:VT, 0:KD], ct[a][:, t // VTC, j // 3, s], w["wv"][v][:, j // 3, :],
                                       start=(j == 0), stop=(j == 3 * KT - 1))
                    if part == 1:
                        mm.then_inc(proj_done, 1)

                def max_scores(b, p):
                    if p == 0:
                        pe.wait_ge(qk_loaded, b * 160 + 160)
                        pe.wait_ge(exp_done, START + b * NU)
                    pe.wait_ge(max_done, START + b * PARTS + max(p - 1, 0))
                    h = p // 2
                    first, N = MAXCOLS[p % 2]
                    for i in range(2):
                        mm = pe.matmul(psc[0:HALF, 2 * (p % 2) + i, 0:N], q[0][0:HD, h * HALF:(h + 1) * HALF],
                                       kt[0][:, h // 2, first + i * N:first + (i + 1) * N], start=True, stop=True)
                    mm.then_inc(maxmm_done, 1)

                def spread_max(b):
                    pe.wait_ge(mdiag_done, 2 * b + 2)
                    pe.wait_ge(o_copied, START + b * KV)
                    pe.wait_ge(z_inverted, START + b * H)
                    for i in range(2):
                        mm = pe.matmul(pav[:, i, 0:KV * HALF], ones[:], mdiag[:, i, :], start=True, stop=True)
                    mm.then_inc(mb_done, 1)

                def scores(b, u):
                    h, j = u // UNITS, u % UNITS
                    if u < SBANKS:
                        pe.wait_ge(max_done, START + b * PARTS + PARTS)
                    else:
                        pe.wait_ge(exp_done, START + b * NU + u - SBANKS + 1)
                    tiles = (2 * j, 2 * j + 1) if j < UNITS - 1 else (NVT,)
                    for n, t in enumerate(tiles):
                        s = slice(t * VT, min((t + 1) * VT, SL))
                        R = s.stop - s.start
                        o = psc[0:R, u % SBANKS, n * GQ:(n + 1) * GQ]
                        c = slice(h * GQ, (h + 1) * GQ)
                        pe.matmul(o, kt[0][:, h, s], q[0][0:HD, c], start=True, stop=False)
                        pe.matmul(o, kt[0][:, h, s], q[1][:, c], start=False, stop=False)
                        if u == 0 and n == 0:
                            pe.wait_ge(mneg_done, b + 1)
                        mm = pe.matmul(o, kt[1][:, h, s], q[0][:, c], start=False, stop=True)
                    mm.then_inc(scores_done, 1)

                def weigh(b, u):
                    h, j = u // UNITS, u % UNITS
                    pe.wait_ge(p_lo, START + b * NU + u + 1)
                    if u == 0:
                        pe.wait_ge(v_loaded, b * 32 + 32)
                    if h == 0 and j < UNITS - 1:
                        pe.wait_ge(proj_lo, START + b * NPROJ + CHUNKS * KTILES + 2 * j + 2)
                    if j == 0 and h >= 2:
                        pe.wait_ge(o_copied, START + b * KV + h - 1)
                        pe.wait_ge(z_inverted, START + b * H + (h - 1) * G)
                    tiles = (2 * j, 2 * j + 1) if j < UNITS - 1 else (NVT,)
                    for n, t in enumerate(tiles):
                        R = VT if t < NVT else Q
                        c = slice(n * GQ, (n + 1) * GQ)
                        o = pav[0:HD + 1, h % 2, 0:GQ]
                        hi, lo = (x[0:R, u % PRING, c] for x in prs)
                        pe.matmul(o, vt_hi[0:R, t, h], hi, start=(t == 0), stop=False)
                        pe.matmul(pav[0:HD, h % 2, 0:GQ], vt_lo[0:R, t, h], hi, start=False, stop=False)
                        mm = pe.matmul(o, vt_hi[0:R, t, h], lo, start=False, stop=(t == NVT))
                    mm.then_inc(pv_done, 1)

                with pe.Fori(0, B) as b:
                    for c in range(CHUNKS):
                        for i in range(KTILES):
                            project_keys(b, c, i)
                    for t in range(NVT):
                        for part in range(2):
                            project_values(b, t, part)
                            if 2 * t + part < PARTS:
                                max_scores(b, 2 * t + part)
                        if t == NVT - 3:
                            spread_max(b)
                        if t == NVT - 2:
                            scores(b, 0)
                            scores(b, 1)
                    for u in range(2, AHEAD):
                        scores(b, u)
                    for u in range(NU):
                        if u + AHEAD < NU:
                            scores(b, u + AHEAD)
                        weigh(b, u)


def combine(nc, wo, io, scratch):
    with ExitStack() as ctx:
        sb = lambda name, shape, dt=F32: ctx.enter_context(nc.sbuf_tensor(name, shape, dt))
        sem = lambda name: ctx.enter_context(nc.semaphore(name))
        wg = sb("w_gate", [P, KT, E])
        bg = sb("b_gate", [1, E])
        ones = sb("ones_g", [1, P])
        ident = sb("ident_g", [P, P])
        iota_u = sb("iota_u", [P, E], mybir.dt.int32)
        iota = sb("iota_f", [P, E])
        eps = sb("eps_g", [P, 1])
        att = sb("att", [P, 2, HT, P])
        rz = sb("inv_sums", [P, 2, HT, P])
        an = sb("att_scaled", [P, HT, P])
        ats = [sb(f"att_{n}", [P, 2, HT, P], F32R) for n in ("hi", "lo")]
        x = sb("x_rows", [P, 2, D])
        x1 = sb("x1", [P, 2, D + E])
        stats, mv, std, rstd = sb("stats_g", [P, 6]), sb("mv_g", [P, 2]), sb("std_g", [P, 1]), sb("rstd_g", [P, 1])
        xn = sb("xn_g", [P, D])
        xt = sb("xt_g", [P, 2, KT, P])
        lg = sb("logits", [P, E])
        top, topi = sb("top", [P, E]), sb("top_index", [P, E], U32)
        topf = sb("top_index_f", [P, E])
        sel = sb("selected", [P, 2, E])
        po = [ctx.enter_context(nc.psum_tensor(f"ps_o{i}", [P, D], F32)) for i in range(2)]
        pt = ctx.enter_context(nc.psum_tensor("ps_t", [P, KT, P], F32))
        pg = ctx.enter_context(nc.psum_tensor("ps_g", [P, E], F32))

        loaded = [sem(f"rows_loaded{i}") for i in range(2)]
        x_loaded = [sem(f"x_rows_loaded{i}") for i in range(2)]
        small_loaded, consts = sem("small_loaded"), sem("consts_g")
        scaled, a_hi, a_lo = sem("att_scaled_done"), sem("att_hi_ready"), sem("att_lo_ready")
        o_done, x1_done = sem("o_done"), sem("x1_done")
        waited = sem("waited_g")
        stats_done, aggregated, std_done, rstd_done = sem("stats_done_g"), sem("aggregated"), sem("std_done_g"), sem("rstd_done_g")
        normed = sem("normed_g")
        logits_ready, top_ready, index_ready = sem("logits_ready"), sem("top_ready"), sem("index_ready")
        index_f_ready, sel_ready = sem("index_f_ready"), sem("sel_ready")
        turned, xt_done, g_done, gate_done = sem("turned_g"), sem("xt_ready"), sem("gate_logits"), sem("gate_done")
        stored = [sem(f"rows_stored{i}") for i in range(2)]
        att_v = scratch["att"].rearrange("(k p) r -> p k r", p=P)
        x_v = io["x"].rearrange("(t r) d -> t r d", r=P)
        ROW_LOADS = 16 * (1 + len(HEAD_PIECES))

        with nc.Block() as block:
            @block.sync
            def _(sp):
                for s in stored:
                    sp.sem_inc(s, START)
                def load(t, s):
                    cols = bass.ds(t * P, P)
                    sp.dma_start(att[:, s], att_v[:, :, cols]).then_inc(loaded[s], 16)
                    for k, p0, n, h in HEAD_PIECES:
                        src = scratch["rz"][:, cols].rearrange("(a h) r -> h a r", h=4)[h:h + 1]
                        sp.dma_start(rz[p0:p0 + n, s].rearrange("p (a k) r -> p a k r", k=3)[:, :, k, :],
                                     src.broadcast_to([n, HT // 3, P])).then_inc(loaded[s], 16)

                def load_x(t, s):
                    sp.dma_start(x[:, s], x_v[t]).then_inc(x_loaded[s], 16)

                def store(t, s):
                    sp.wait_ge(xt_done, t + 1)
                    sp.dma_start(scratch["xt"][t], xt[:, s]).then_inc(stored[s], 16)
                    sp.wait_ge(gate_done, t + 1)
                    sp.dma_start(scratch["x1"][t], x1[:, s]).then_inc(stored[s], 16)

                load(0, 0)
                load_x(0, 0)
                sp.dma_start(wg[:], io["wg"]).then_inc(small_loaded, 16)
                sp.dma_start(bg[:], io["bg"]).then_inc(small_loaded, 16)
                load(1, 1)
                load_x(1, 1)

                def tile(t, s, more=True, first=False):
                    if more:
                        sp.wait_ge(scaled, t + 1)
                        load(t + 2, s)
                        sp.wait_ge(x1_done, t + 1)
                        load_x(t + 2, s)
                    if not first:
                        store(t - 1, 1 - s)

                tile(0, 0, first=True)
                with sp.Fori(0, OT // 2 - 2) as i:
                    for s in (1, 0):
                        tile(2 * i + 2 - s, s)
                tile(OT - 3, 1)
                tile(OT - 2, 0, more=False)
                tile(OT - 1, 1, more=False)
                store(OT - 1, 1)
                for s in range(2):
                    sp.wait_ge(stored[s], START + 32 * OT // 2)

            @block.gpsimd
            def _(pool):
                pool.memset(eps[:], EPS).then_inc(consts, 1)
                pool.memset(ones[:], 1.0).then_inc(consts, 1)
                pool.memset(ident[:], 0.0).then_inc(consts, 1)
                pool.iota(iota_u[:], pattern=[[1, E]], base=0, channel_multiplier=0).then_inc(consts, 1)
                pool.wait_ge(consts, 4)
                pool.affine_select(out=ident[:], in_=ident[:], compare_op=ALU.not_equal, fill=1.0, base=0,
                                   pattern=[[-1, P]], channel_multiplier=1).then_inc(consts, 1)
                pool.tensor_copy(iota[:], iota_u[:]).then_inc(consts, 1)

                with pool.Fori(0, OT // 2) as i:
                    for s in range(2):
                        t = 2 * i + s
                        pool.wait_ge(loaded[s], i * ROW_LOADS + ROW_LOADS)
                        pool.wait_ge(a_lo, START + t)
                        pool.tensor_tensor(an[:], att[:, s], rz[:, s], ALU.mult).then_inc(scaled, 1)

            @block.scalar
            def _(act):
                act.wait_ge(consts, 6)

                def split(t, s):
                    act.wait_ge(scaled, t + 1)
                    act.wait_ge(o_done, START + t - 1)
                    act.copy(ats[0][:, s], an[:]).then_inc(a_hi, 1)

                def deviation(t):
                    act.wait_ge(aggregated, t + 1)
                    act.activation(std[:], mv[:, 1:2], ACT.Sqrt, bias=eps[:]).then_inc(std_done, 1)

                def turn(t, s):
                    act.wait_ge(turned, START + t + 1)
                    act.wait_ge(stored[s], START + (t - s) * 16)
                    act.copy(xt[:, s], pt[:]).then_inc(xt_done, 1)

                def finish(t, s, more):
                    deviation(t)
                    if more:
                        split(t + 2, s)
                    turn(t, s)

                act.wait_ge(scaled, 1)
                act.copy(ats[0][:, 0], an[:]).then_inc(a_hi, 1)
                split(1, 1)
                with act.Fori(0, OT // 2 - 1) as i:
                    for s in range(2):
                        finish(2 * i + s, s, True)
                for s in range(2):
                    finish(OT - 2 + s, s, False)

            @block.vector
            def _(dve):
                for s in (a_lo, logits_ready):
                    dve.sem_inc(s, START)
                dve.wait_ge(consts, 6)

                def split(t, s):
                    dve.wait_ge(a_hi, t + 1)
                    dve.tensor_tensor(ats[1][:, s], an[:], f(ats[0][:, s]), ALU.subtract).then_inc(a_lo, 1)

                def norm(t, s):
                    dve.wait_ge(o_done, START + t + 1)
                    dve.wait_ge(x_loaded[s], (t - s) * 8 + 16)
                    dve.wait_ge(stored[s], START + (t - s) * 16)
                    dve.tensor_tensor(x1[:, s, 0:D], po[s][:], x[:, s], ALU.add).then_inc(x1_done, 1)
                    dve.wait_ge(x1_done, t + 1)
                    dve.bn_stats(stats[:], x1[:, s, 0:D]).then_inc(stats_done, 1)
                    wait_apart(dve, stats_done, t + 1, waited)
                    dve.bn_aggr(mv[:], stats[:]).then_inc(aggregated, 1)
                    dve.wait_ge(std_done, t + 1)
                    dve.reciprocal(rstd[:], std[:]).then_inc(rstd_done, 1)
                    dve.wait_ge(rstd_done, t + 1)
                    dve.wait_ge(turned, START + t)
                    dve.tensor_scalar(xn[:], x1[:, s, 0:D], mv[:, 0:1], rstd[:], ALU.subtract, ALU.mult).then_inc(normed, 1)

                def gate(t, s):
                    dve.wait_ge(g_done, t + 1)
                    dve.tensor_copy(lg[:], pg[:]).then_inc(logits_ready, 1)
                    wait_apart(dve, logits_ready, START + t + 1, waited)
                    dve.max(top[:], lg[:]).then_inc(top_ready, 1)
                    wait_apart(dve, top_ready, t + 1, waited)
                    dve.max_index(topi[:], top[:], lg[:]).then_inc(index_ready, 1)
                    dve.wait_ge(index_ready, t + 1)
                    dve.tensor_copy(topf[:], topi[:]).then_inc(index_f_ready, 1)
                    dve.wait_ge(index_f_ready, t + 1)
                    for n in range(2):
                        dve.tensor_scalar(sel[:, n, :], iota[:], topf[:, n:n + 1], 0.5, ALU.is_equal, ALU.mult).then_inc(sel_ready, 1)
                    dve.wait_ge(sel_ready, 2 * t + 2)
                    dve.tensor_tensor(x1[:, s, D:D + E], sel[:, 0, :], sel[:, 1, :], ALU.add).then_inc(gate_done, 1)

                def finish(t, s, more):
                    norm(t, s)
                    if more:
                        split(t + 2, s)
                    gate(t, s)

                for t in range(2):
                    split(t, t)
                with dve.Fori(0, OT // 2 - 1) as i:
                    for s in range(2):
                        finish(2 * i + s, s, True)
                for s in range(2):
                    finish(OT - 2 + s, s, False)

            @block.tensor
            def _(pe):
                for s in (o_done, turned):
                    pe.sem_inc(s, START)
                pe.wait_ge(consts, 6)
                pe.wait_ge(small_loaded, 32)

                def turn(t):
                    pe.wait_ge(normed, t + 1)
                    for k in range(KT):
                        mm = pe.transpose(pt[:, k, :], xn[:, k * P:(k + 1) * P], ident[:])
                    mm.then_inc(turned, 1)

                def logits(t, s):
                    pe.wait_ge(xt_done, t + 1)
                    pe.wait_ge(logits_ready, START + t)
                    for k in range(KT):
                        pe.matmul(pg[:], xt[:, s, k, :], wg[:, k, :], start=(k == 0), stop=False)
                    pe.matmul(pg[:], ones[:], bg[:], start=False, stop=True).then_inc(g_done, 1)

                def output(t, s, first=False):
                    pe.wait_ge(a_lo, START + t + 1)
                    n = 3 * HT
                    for j in range(n):
                        mm = pe.matmul(po[s][:], ats[TERMS[j % 3][0]][:, s, j // 3, :], wo[TERMS[j % 3][1]][:, j // 3, :],
                                       start=(j == 0), stop=(j == n - 1))
                        if not first and j == n // 2:
                            turn(t - 1)
                        if not first and j == 3 * n // 4:
                            logits(t - 1, 1 - s)
                    mm.then_inc(o_done, 1)

                output(0, 0, first=True)
                with pe.Fori(0, OT // 2 - 1) as i:
                    for s in (1, 0):
                        output(2 * i + 2 - s, s)
                output(OT - 1, 1)
                turn(OT - 1)
                logits(OT - 1, 1)


def experts(nc, io, scratch, out_d):
    with ExitStack() as ctx:
        sb = lambda name, shape, dt=F32: ctx.enter_context(nc.sbuf_tensor(name, shape, dt))
        sem = lambda name: ctx.enter_context(nc.semaphore(name))
        BANKS, YRING = 4, 2
        we_raw = sb("we_raw", [P, 2, KT, D])
        we = [sb(f"we_{n}", [P, E, KT, D], F32R) for n in ("hi", "lo")]
        be_raw = sb("be_raw", [E, D])
        be_lo = sb("be_lo", [E, D], F32R)
        be = sb("be", [2 * E, D], F32R)
        pick_f = sb("pick_f", [2 * E, E, P])
        pick = sb("pick", [2 * E, E, P], F32R)
        xt = sb("xt_e", [P, 2, KT, P])
        xs = [sb(f"xs_{n}", [P, 2, KT, P], F32R) for n in ("hi", "lo")]
        x1 = sb("x1_e", [P, 2, D + E])
        y = sb("y", [P, YRING, D])
        acc = sb("acc", [P, 2, D])
        po = [ctx.enter_context(nc.psum_tensor(f"ps_e{i}", [P, D], F32)) for i in range(BANKS)]

        w_loaded = [sem(f"we_loaded{i}") for i in range(2)]
        b_loaded, b_moved = sem("be_loaded"), sem("be_moved")
        loaded = [sem(f"tile_loaded{i}") for i in range(2)]
        consts = sem("consts_e")
        w_hi, w_lo, b_hi, b_lo = sem("we_hi_ready"), sem("we_lo_ready"), sem("be_hi_ready"), sem("be_lo_ready")
        x_hi, x_lo = sem("xs_hi_ready"), sem("xs_lo_ready")
        e_done, relu_done, acc_done = sem("expert_done"), sem("relu_done"), sem("acc_done")
        stored = [sem(f"out_stored{i}") for i in range(2)]
        out_v = out_d.rearrange("(t r) d -> t r d", r=P)

        with nc.Block() as block:
            @block.sync
            def _(sp):
                for s in stored:
                    sp.sem_inc(s, START)
                def load(t, s):
                    sp.dma_start(xt[:, s], scratch["xt"][t]).then_inc(loaded[s], 16)
                    sp.dma_start(x1[:, s], scratch["x1"][t]).then_inc(loaded[s], 16)

                load(0, 0)
                sp.dma_start(be_raw[:], io["be"]).then_inc(b_loaded, 16)
                for e in range(E):
                    if e >= 2:
                        sp.wait_ge(w_lo, e - 1)
                    sp.dma_start(we_raw[:, e % 2], io["we"][:, e]).then_inc(w_loaded[e % 2], 16)
                    if e == 1:
                        load(1, 1)
                        sp.wait_ge(b_lo, 1)
                        sp.dma_start(f(be[E:2 * E, :]), f(be_lo[:])).then_inc(b_moved, 16)

                def tile(t, s, more):
                    sp.wait_ge(acc_done, YRING + t * E + E)
                    if more:
                        load(t + 2, s)
                    sp.dma_start(out_v[t], acc[:, s]).then_inc(stored[s], 16)

                with sp.Fori(0, OT // 2 - 1) as i:
                    for s in range(2):
                        tile(2 * i + s, s, True)
                for s in range(2):
                    tile(OT - 2 + s, s, False)
                for s in range(2):
                    sp.wait_ge(stored[s], START + 16 * OT // 2)

            @block.gpsimd
            def _(pool):
                pool.memset(pick_f[:], 0.0).then_inc(consts, 1)
                for n in range(2):
                    pool.wait_ge(consts, n + 1)
                    pool.affine_select(out=pick_f[:], in_=pick_f[:], compare_op=ALU.not_equal, fill=1.0, base=-E * n,
                                       pattern=[[-1, E], [0, P]], channel_multiplier=1).then_inc(consts, 1)

            @block.scalar
            def _(act):
                act.sem_inc(relu_done, BANKS)
                def split(t, i, s):
                    act.wait_ge(loaded[s], i * 32 + 32)
                    act.copy(xs[0][:, s], xt[:, s]).then_inc(x_hi, 1)

                def split_w(e):
                    act.wait_ge(w_loaded[e % 2], 16 * (e // 2) + 16)
                    act.copy(we[0][:, e], we_raw[:, e % 2]).then_inc(w_hi, 1)

                split(0, 0, 0)
                split_w(0)
                act.wait_ge(b_loaded, 16)
                act.copy(be[0:E, :], be_raw[:]).then_inc(b_hi, 1)
                split_w(1)

                def tile(i, s, more, first=False):
                    t = 2 * i + s
                    for e in range(E):
                        if first and e + 2 < E:
                            split_w(e + 2)
                        act.wait_ge(e_done, t * E + e + 1)
                        act.wait_ge(acc_done, t * E + e + 1)
                        act.activation(y[:, e % YRING], po[e % BANKS][:], ACT.Relu, scale=x1[:, s, D + e:D + e + 1]).then_inc(relu_done, 1)
                        if e == 2 and more:
                            split(t + 1, i + s, 1 - s)

                for s in range(2):
                    tile(0, s, True, first=(s == 0))
                with act.Fori(1, OT // 2 - 1) as i:
                    for s in range(2):
                        tile(i, s, True)
                for s in range(2):
                    tile(OT // 2 - 1, s, s == 0)

            @block.vector
            def _(dve):
                dve.sem_inc(acc_done, YRING)
                def split(t, s):
                    dve.wait_ge(x_hi, t + 1)
                    dve.tensor_tensor(xs[1][:, s], xt[:, s], f(xs[0][:, s]), ALU.subtract).then_inc(x_lo, 1)

                split(0, 0)
                dve.wait_ge(b_hi, 1)
                dve.tensor_tensor(be_lo[:], be_raw[:], f(be[0:E, :]), ALU.subtract).then_inc(b_lo, 1)
                dve.wait_ge(consts, 3)
                dve.tensor_copy(pick[:], pick_f[:]).then_inc(consts, 1)
                def split_w(e):
                    dve.wait_ge(w_hi, e + 1)
                    dve.tensor_tensor(we[1][:, e], we_raw[:, e % 2], f(we[0][:, e]), ALU.subtract).then_inc(w_lo, 1)

                for e in range(2):
                    split_w(e)

                def tile(i, s, more, first=False):
                    t = 2 * i + s
                    dve.wait_ge(stored[s], START + 16 * i)
                    for e in range(E):
                        if first and e + 2 < E:
                            split_w(e + 2)
                        dve.wait_ge(relu_done, BANKS + t * E + e + 1)
                        dve.wait_ge(acc_done, YRING + t * E + e)
                        dve.tensor_tensor(acc[:, s], x1[:, s, 0:D] if e == 0 else acc[:, s], y[:, e % YRING], ALU.add).then_inc(acc_done, 1)
                        if e == 2 and more:
                            split(t + 1, 1 - s)

                for s in range(2):
                    tile(0, s, True, first=(s == 0))
                with dve.Fori(1, OT // 2 - 1) as i:
                    for s in range(2):
                        tile(i, s, True)
                for s in range(2):
                    tile(OT // 2 - 1, s, s == 0)

            @block.tensor
            def _(pe):
                pe.wait_ge(consts, 4)
                with pe.Fori(0, OT // 2) as i:
                    for s in range(2):
                        t = 2 * i + s
                        pe.wait_ge(x_lo, t + 1)
                        for e in range(E):
                            pe.wait_ge(w_lo, e + 1)
                            pe.wait_ge(relu_done, t * E + e + 1)
                            for j in range(3 * KT):
                                a, v = TERMS[j % 3]
                                pe.matmul(po[e % BANKS][:], xs[a][:, s, j // 3, :], we[v][:, e, j // 3, :], start=(j == 0), stop=False)
                            if e == 0:
                                pe.wait_ge(b_moved, 16)
                            pe.matmul(po[e % BANKS][:], pick[:, e, :], be[:], start=False, stop=True).then_inc(e_done, 1)


def build(nc, io, out_d):
    scratch = {
        "qk": [nc.dram_tensor(f"qk_{n}", (HH + KD, ROWS), F32, kind="Internal").ap() for n in ("hi", "lo")],
        "v": [nc.dram_tensor(f"v_{n}", (ROWS, KD), F32, kind="Internal").ap() for n in ("hi", "lo")],
        "att": nc.dram_tensor("att_t", (HH, ROWS), F32, kind="Internal").ap(),
        "rz": nc.dram_tensor("inverse_sums", (H, ROWS), F32, kind="Internal").ap(),
        "x1": nc.dram_tensor("x1_gate", (OT, P, D + E), F32, kind="Internal").ap(),
        "xt": nc.dram_tensor("xt_normed", (OT, P, KT * P), F32, kind="Internal").ap(),
    }
    scratch["xt"] = scratch["xt"].rearrange("t p (k r) -> t p k r", k=KT)
    with ExitStack() as ctx:
        w = {name: [ctx.enter_context(nc.sbuf_tensor(f"{name}_{n}", [P, KT, KD], F32R)) for n in ("hi", "lo")]
             for name in ("wk", "wv")}
        parts = ctx.enter_context(nc.sbuf_tensor("parts", [P, 2, HT * D], F32R))
        wo = [parts[:, i].rearrange("p (t d) -> p t d", d=D) for i in range(2)]
        raw = ctx.enter_context(nc.sbuf_tensor("raw", [P, RAW, WOT * D], F32))
        sem = lambda name: ctx.enter_context(nc.semaphore(name))
        stream = {
            "raw_full": raw, "raw": raw[:, :, 0:KH * CS].rearrange("p n (k s) -> p n k s", s=CS), "wo": wo,
            "parts": [parts[:, i, 0:CHUNKS * KT * CS].rearrange("p (c k s) -> p c k s", c=CHUNKS, k=KT) for i in range(2)],
            "loaded": [sem(f"ctx_loaded{i}") for i in range(RAW)],
            "hi": sem("ctx_hi_ready"), "lo": sem("ctx_lo_ready"), "waited": sem("ctx_waited"),
        }
        project(nc, w, stream, io, scratch)
        attend(nc, w, stream, io, scratch)
        combine(nc, wo, io, scratch)
    experts(nc, io, scratch, out_d)


def kernel(x, ctx_4096, L0_xattn_Wq, L0_xattn_Wk, L0_xattn_Wv, L0_xattn_Wo, L0_ffn_W_gate, L0_ffn_b_gate,
           L0_ffn_W_e, L0_ffn_b_e):
    import numpy as np
    import concourse.bacc as bacc
    from concourse.bass_utils import run_bass_kernel_spmd

    def stationary(w):
        return w.T.reshape(-1, P, w.shape[0]).transpose(1, 0, 2)

    wk = np.asarray(L0_xattn_Wk)
    last = wk[KTILES * HD:]
    wk_tiles = np.concatenate([part for i in range(KTILES)
                               for part in (wk[i * HD:(i + 1) * HD], last[i * PIECE:(i + 1) * PIECE])])
    arrays = {
        "x": np.asarray(x).reshape(ROWS, D),
        "ctx": np.asarray(ctx_4096).reshape(B, CHUNKS, CS, KT, P).transpose(0, 1, 4, 3, 2),
        "wq": stationary(np.asarray(L0_xattn_Wq)),
        "wk": stationary(wk_tiles),
        "wv": stationary(np.asarray(L0_xattn_Wv)),
        "wo": stationary(np.asarray(L0_xattn_Wo)),
        "wg": np.asarray(L0_ffn_W_gate).reshape(KT, P, E).transpose(1, 0, 2),
        "bg": np.asarray(L0_ffn_b_gate).reshape(1, E),
        "we": np.asarray(L0_ffn_W_e).reshape(E, KT, P, D).transpose(2, 0, 1, 3),
        "be": np.asarray(L0_ffn_b_e),
    }
    arrays = {k: np.ascontiguousarray(v) for k, v in arrays.items()}
    nc = bacc.Bacc("TRN2", target_bir_lowering=False, num_devices=1)
    io = {k: nc.dram_tensor(f"in_{k}", v.shape, F32, kind="ExternalInput").ap() for k, v in arrays.items()}
    out_d = nc.dram_tensor("out", (ROWS, D), F32, kind="ExternalOutput").ap()
    build(nc, io, out_d)
    r = run_bass_kernel_spmd(nc, [{f"in_{k}": v for k, v in arrays.items()}], core_ids=[0])
    return r.results[0]["out"].reshape(B, Q, D)
```

```python
from contextlib import ExitStack

import concourse.bass as bass
from concourse import mybir

F32 = mybir.dt.float32
F32R = mybir.dt.float32r
U32 = mybir.dt.uint32
ALU = mybir.AluOpType
ACT = mybir.ActivationFunctionType
AX = mybir.AxisListType

P = 128
B, Q, D = 32, 56, 512
S = 1500
H, KV, HD = 16, 4, 96
G = H // KV
E = 8
EPS = 1e-5
SCALE = float(HD) ** -0.5
KT = D // P
ROWS = B * Q
SL = S + Q
GQ = G * Q
KD = KV * HD
HH = H * HD

PIECE = P - HD
KTILES = KD // P
CHUNKS = 3
CS = S // CHUNKS
HALVES_C = 2
KH = KT // HALVES_C
LOADS = CHUNKS * HALVES_C
RAW = 3
VT = 125
VTC = CS // VT
NVT = S // VT

GROUPS = 4
GR = ROWS // GROUPS
RT = 112
GT = GR // RT
MQ = HH // P
MK = MQ + KTILES
NOUT = MK + GT
WQP = HH // KD
OSLOTS, OBANKS = 3, 4

HALVES = 2 * KV
HALF = GQ // 2
MAXCOLS = [(0, 390), (780, 388)]
PARTS = 2 * HALVES
UNITS = 7
NU = KV * UNITS
SBANKS = 4
AHEAD = 3
PRING = 4
NPROJ = CHUNKS * KTILES + NVT
NHI = 2 * CHUNKS * KTILES + NVT

OT = ROWS // P
HT = HH // P
WOT = HT // LOADS
EARLY = 1
LATE = E - EARLY
SPLIT_TILES = (OT - 6, OT - 5)
RAW_E = 3
HEAD_PIECES = [(0, 0, 96, 0), (0, 96, 32, 1), (1, 0, 64, 1), (1, 64, 64, 2), (2, 0, 32, 2), (2, 32, 96, 3)]
ROW_LOADS = 16 * (1 + len(HEAD_PIECES))


START = 1
TERMS = ((0, 0), (0, 1), (1, 0))


def wait_apart(eng, sem, value, waited):
    eng.wait_ge(sem, value)
    eng.sem_inc(waited, 1)


def f(ap):
    return ap.bitcast(F32)


def load_ctx(sp, stream, io, b, n, first=False):
    if not (first and n < RAW):
        sp.wait_ge(stream["lo"], b * LOADS + n - RAW + 1)
    k = n % HALVES_C * KH
    sp.dma_start(stream["raw"][:, n % RAW], io["ctx"][b, n // HALVES_C, :, k:k + KH, :]).then_inc(stream["loaded"][n % RAW], 16)


def split(pool, stream, b, n, raw, parts):
    wait_apart(pool, stream["loaded"][n % RAW], b * 32 + n // RAW * 16 + 16, stream["waited"])
    hi, lo = parts
    pool.tensor_scalar(hi, raw, 1.0, 0.0, ALU.mult, ALU.add).then_inc(stream["hi"], 1)
    pool.wait_ge(stream["hi"], b * LOADS + n + 1)
    pool.tensor_tensor(lo, raw, f(hi), ALU.subtract).then_inc(stream["lo"], 1)


def split_ctx(pool, stream, b, n):
    c, k = n // HALVES_C, n % HALVES_C * KH
    split(pool, stream, b, n, stream["raw"][:, n % RAW], [p[:, c, k:k + KH] for p in stream["parts"]])


def load_wo(sp, stream, io, n):
    sp.wait_ge(stream["lo"], B * LOADS + n - RAW + 1)
    raw = stream["raw_full"][:, n % RAW].rearrange("p (t d) -> p t d", d=D)
    sp.dma_start(raw, io["wo"][:, n * WOT:(n + 1) * WOT]).then_inc(stream["loaded"][n % RAW], 16)


def split_wo(pool, stream, n):
    split(pool, stream, B, n, stream["raw_full"][:, n % RAW].rearrange("p (t d) -> p t d", d=D),
          [p[:, n * WOT:(n + 1) * WOT] for p in stream["wo"]])


def load_rows(sp, scratch, t, att, rz, loaded):
    cols = bass.ds(t * P, P)
    sp.dma_start(att, scratch["att"].rearrange("(k p) r -> p k r", p=P)[:, :, cols]).then_inc(loaded, 16)
    for k, p0, n, h in HEAD_PIECES:
        src = scratch["rz"][:, cols].rearrange("(a h) r -> h a r", h=4)[h:h + 1]
        sp.dma_start(rz[p0:p0 + n].rearrange("p (a k) r -> p a k r", k=3)[:, :, k, :],
                     src.broadcast_to([n, HT // 3, P])).then_inc(loaded, 16)


def load_normed(sp, scratch, early, t, s):
    sp.dma_start(early["xt"][:, s], scratch["xt"][t]).then_inc(early["tile_loaded"][s], 16)
    sp.dma_start(early["x1"][:, s], scratch["x1"][t]).then_inc(early["tile_loaded"][s], 16)


def project(nc, w, stream, io, scratch):
    with ExitStack() as ctx:
        sb = lambda name, shape, dt=F32: ctx.enter_context(nc.sbuf_tensor(name, shape, dt))
        sem = lambda name: ctx.enter_context(nc.semaphore(name))
        w_raw = sb("w_raw", [P, 2, KT, KD])
        wq = [sb(f"wq_{n}", [P, KT, HH], F32R) for n in ("hi", "lo")]
        x = sb("x_group", [RT, GT, D])
        xn = sb("x_normed", [RT, GT, D])
        stats = sb("ln_stats", [RT, GT, 6])
        mv = sb("ln_mean_var", [RT, GT, 2])
        std = sb("ln_std", [RT, GT])
        rstd = sb("ln_rstd", [RT, GT])
        eps = sb("eps_p", [P, 1])
        ident = sb("ident_p", [P, P])
        xt = [sb(f"xt_{n}", [P, KT, GR], F32R) for n in ("hi", "lo")]
        out = [sb(f"proj_out_{n}", [P, OSLOTS, GR], F32R) for n in ("hi", "lo")]
        pt = [ctx.enter_context(nc.psum_tensor(f"ps_xt{i}", [P, GR], F32)) for i in range(KT)]
        po = [ctx.enter_context(nc.psum_tensor(f"ps_out{i}", [P, GR], F32)) for i in range(OBANKS)]

        waited = sem("waited_p")
        x_loaded = sem("x_loaded")
        first_loaded = [sem(f"first_rows_loaded{t}") for t in range(GT)]
        w_loaded = [sem(f"w_loaded{i}") for i in range(2)]
        consts = sem("consts_ready")
        stats_done, mv_done, std_done, rstd_done = sem("stats_done"), sem("mv_done"), sem("std_done"), sem("rstd_done")
        normed = sem("normed")
        turned = sem("turned")
        xt_hi, xt_lo = sem("xt_hi_ready"), sem("xt_lo_ready")
        w_hi, w_lo = sem("w_hi_ready"), sem("w_lo_ready")
        out_done = sem("out_done")
        out_hi, out_lo = sem("out_hi_ready"), sem("out_lo_ready")
        stored = [sem(f"stored{i}") for i in range(OSLOTS)]
        xg = io["x"].rearrange("(g t r) d -> g r t d", t=GT, r=RT)
        qk_d = [s.rearrange("m (g c) -> g m c", c=GR) for s in scratch["qk"]]
        v_d = [s.rearrange("(g t r) n -> g t r n", t=GT, r=RT) for s in scratch["v"]]
        cols = lambda i: slice(i * KD, (i + 1) * KD)
        w_from = [io["wq"][:, :, cols(i)] for i in range(WQP)] + [io["wk"], io["wv"]]
        w_to = [[t[:, :, cols(i)] for t in wq] for i in range(WQP)] + [[t[:] for t in w[n]] for n in ("wk", "wv")]

        def uses(i):
            return len(range(i, NOUT, OSLOTS))

        with nc.Block() as block:
            @block.sync
            def _(sp):
                for s in stored:
                    sp.sem_inc(s, START)
                for t in range(GT):
                    sp.dma_start(x[:, t], xg[0][:, t]).then_inc(first_loaded[t], 16)

                def load_w(i):
                    if i >= 2:
                        sp.wait_ge(w_lo, i - 1)
                    sp.dma_start(w_raw[:, i % 2], w_from[i]).then_inc(w_loaded[i % 2], 16)

                for i in range(4):
                    load_w(i)

                def group(g, more, first=False):
                    if more:
                        sp.wait_ge(normed, g * GT + GT)
                        sp.dma_start(x[:], xg[g + 1]).then_inc(x_loaded, 16)
                    for n in range(NOUT):
                        if not more and n < 3 * LOADS and n % 3 == 0:
                            load_ctx(sp, stream, io, 0, n // 3, first=True)
                        sp.wait_ge(out_lo, START + g * NOUT + n + 1)
                        for i in range(2):
                            if n < MK:
                                src, dst = f(out[i][:, n % OSLOTS, :]), qk_d[i][g, n * P:(n + 1) * P]
                            else:
                                src, dst = f(out[i][0:RT, n % OSLOTS, 0:KD]), v_d[i][g, n - MK]
                            sp.dma_start(dst, src).then_inc(stored[n % OSLOTS], 16)
                        if first and n in (2, 5):
                            load_w(n // 3 + 4)

                group(0, True, first=True)
                with sp.Fori(1, GROUPS - 1) as g:
                    group(g, True)
                group(GROUPS - 1, False)
                for i in range(OSLOTS):
                    sp.wait_ge(stored[i], START + 32 * GROUPS * uses(i))

            @block.gpsimd
            def _(pool):
                pool.memset(eps[:], EPS).then_inc(consts, 1)
                pool.memset(ident[:], 0.0).then_inc(consts, 1)
                pool.wait_ge(consts, 2)
                pool.affine_select(out=ident[:], in_=ident[:], compare_op=ALU.not_equal, fill=1.0, base=0,
                                   pattern=[[-1, P]], channel_multiplier=1).then_inc(consts, 1)
                for n in range(LOADS):
                    split_ctx(pool, stream, 0, n)

            @block.scalar
            def _(act):
                def norm_scale(g):
                    act.wait_ge(mv_done, g * GT + GT)
                    act.activation(std[:], mv[:, :, 1], ACT.Sqrt, bias=eps[0:RT]).then_inc(std_done, 1)

                def split_out(g, n):
                    act.wait_ge(out_done, START + g * NOUT + n + 1)
                    act.wait_ge(stored[n % OSLOTS], START + g * (32 * uses(n % OSLOTS)) + 32 * (n // OSLOTS))
                    R, N = (P, GR) if n < MK else (RT, KD)
                    act.copy(out[0][0:R, n % OSLOTS, 0:N], po[n % OBANKS][0:R, 0:N]).then_inc(out_hi, 1)

                def turn(g):
                    for k in range(KT):
                        act.wait_ge(turned, START + g * KT + k + 1)
                        if k == 0:
                            act.wait_ge(out_done, START + g * NOUT)
                        act.copy(xt[0][:, k, :], pt[k][:]).then_inc(xt_hi, 1)

                def split_w(i):
                    act.wait_ge(w_loaded[i % 2], 16 * (i // 2) + 16)
                    act.copy(w_to[i][0], w_raw[:, i % 2]).then_inc(w_hi, 1)

                act.wait_ge(consts, 3)
                norm_scale(0)
                split_w(0)
                turn(0)
                split_w(1)

                def group(g, more, first=False):
                    for n in range(NOUT):
                        split_out(g, n)
                        if first and n % KTILES == 1 and n // KTILES + 2 < len(w_to):
                            split_w(n // KTILES + 2)
                        if n == 6 and more:
                            norm_scale(g + 1)
                    if more:
                        turn(g + 1)

                group(0, True, first=True)
                with act.Fori(1, GROUPS - 1) as g:
                    group(g, True)
                group(GROUPS - 1, False)

            @block.vector
            def _(dve):
                for s in (xt_lo, out_lo):
                    dve.sem_inc(s, START)
                def moments(g, first=False):
                    if not first:
                        dve.wait_ge(x_loaded, g * 16)
                    for t in range(GT):
                        if first:
                            wait_apart(dve, first_loaded[t], 16, waited)
                        dve.bn_stats(stats[:, t, :], x[:, t, :]).then_inc(stats_done, 1)
                    for t in range(GT):
                        wait_apart(dve, stats_done, g * GT + t + 1, waited)
                        dve.bn_aggr(mv[:, t, :], stats[:, t, :]).then_inc(mv_done, 1)

                def norm(g):
                    dve.wait_ge(std_done, g + 1)
                    dve.wait_ge(turned, START + g * KT)
                    dve.reciprocal(rstd[:], std[:]).then_inc(rstd_done, 1)
                    dve.wait_ge(rstd_done, g + 1)
                    for t in range(GT):
                        dve.tensor_scalar(xn[:, t, :], x[:, t, :], mv[:, t, 0:1], rstd[:, t:t + 1],
                                          ALU.subtract, ALU.mult).then_inc(normed, 1)

                def split_out(g, n):
                    dve.wait_ge(out_hi, g * NOUT + n + 1)
                    R, N = (P, GR) if n < MK else (RT, KD)
                    dve.tensor_tensor(out[1][0:R, n % OSLOTS, 0:N], po[n % OBANKS][0:R, 0:N],
                                      f(out[0][0:R, n % OSLOTS, 0:N]), ALU.subtract).then_inc(out_lo, 1)

                def turn(g):
                    for k in range(KT):
                        dve.wait_ge(xt_hi, g * KT + k + 1)
                        dve.tensor_tensor(xt[1][:, k, :], pt[k][:], f(xt[0][:, k, :]), ALU.subtract).then_inc(xt_lo, 1)

                def split_w(i):
                    dve.wait_ge(w_hi, i + 1)
                    dve.tensor_tensor(w_to[i][1], w_raw[:, i % 2], f(w_to[i][0]), ALU.subtract).then_inc(w_lo, 1)

                moments(0, first=True)
                norm(0)
                split_w(0)
                turn(0)
                split_w(1)

                def group(g, more, first=False):
                    for n in range(NOUT):
                        split_out(g, n)
                        if first and n % KTILES == 1 and n // KTILES + 2 < len(w_to):
                            split_w(n // KTILES + 2)
                        if n == 4 and more:
                            moments(g + 1)
                        if n == 8 and more:
                            norm(g + 1)
                    if more:
                        turn(g + 1)

                group(0, True, first=True)
                with dve.Fori(1, GROUPS - 1) as g:
                    group(g, True)
                group(GROUPS - 1, False)

            @block.tensor
            def _(pe):
                for s in (turned, out_done):
                    pe.sem_inc(s, START)
                pe.wait_ge(consts, 3)

                def turn(g):
                    pe.wait_ge(normed, g * GT + GT)
                    pe.wait_ge(xt_lo, START + g * KT)
                    for k in range(KT):
                        for t in range(GT):
                            mm = pe.transpose(pt[k][:, t * RT:(t + 1) * RT], xn[:, t, k * P:(k + 1) * P], ident[0:RT, 0:RT])
                        mm.then_inc(turned, 1)

                def product(g, n):
                    pe.wait_ge(out_lo, START + g * NOUT + max(n - OBANKS + 1, 0))
                    last = 3 * KT - 1
                    for j in range(3 * KT):
                        k, (a, b) = j // 3, TERMS[j % 3]
                        if n == 0 and j % 3 == 0:
                            pe.wait_ge(xt_lo, START + g * KT + k + 1)
                        if n < MK:
                            stat = wq[a][:, k, n * P:(n + 1) * P] if n < MQ else w["wk"][a][:, k, (n - MQ) * P:(n - MQ + 1) * P]
                            mm = pe.matmul(po[n % OBANKS][:, :], stat, xt[b][:, k, :], start=(j == 0), stop=(j == last))
                        else:
                            t = n - MK
                            mm = pe.matmul(po[n % OBANKS][0:RT, 0:KD], xt[a][:, k, t * RT:(t + 1) * RT], w["wv"][b][:, k, :],
                                           start=(j == 0), stop=(j == last))
                    mm.then_inc(out_done, 1)

                def group(g, more):
                    for n in range(NOUT):
                        if n % KTILES == 0 and n <= MK:
                            pe.wait_ge(w_lo, n // KTILES + 1)
                        product(g, n)
                        if n == NOUT - 4 and more:
                            turn(g + 1)

                turn(0)
                with pe.Fori(0, GROUPS - 1) as g:
                    group(g, True)
                group(GROUPS - 1, False)


def attend(nc, w, stream, io, scratch):
    with ExitStack() as ctx:
        sb = lambda name, shape, dt=F32: ctx.enter_context(nc.sbuf_tensor(name, shape, dt))
        sem = lambda name: ctx.enter_context(nc.semaphore(name))
        ct = stream["parts"]
        kt = [sb("keys_hi", [HD, KV, SL], F32R), sb("keys_lo", [HD + 1, KV, SL], F32R)]
        vt_hi = sb("values_hi", [VT, NVT + 1, KV, HD + 1], F32R)
        vt_lo = sb("values_lo", [VT, NVT + 1, KV, HD], F32R)
        q = [sb("queries_hi", [HD + 1, KV * GQ], F32R), sb("queries_lo", [HD, KV * GQ], F32R)]
        pr = sb("probs", [VT, PRING, 2 * GQ])
        prs = [sb(f"probs_{n}", [VT, PRING, 2 * GQ], F32R) for n in ("hi", "lo")]
        mpart = sb("max_parts", [HALF, HALVES, 2])
        mrow = sb("max_rows", [HALF, HALVES])
        mdiag = prs[1][0:HALF, 0:2, 0:KV * HALF]
        negident = sb("neg_ident", [HALF, HALF])
        ones = sb("ones_a", [HALF, P], F32R)
        osb = sb("attended", [HD + 1, 2, GQ])
        pproj = [ctx.enter_context(nc.psum_tensor(f"ps_proj{i}", [P, 512], F32)) for i in range(2)]
        psc = ctx.enter_context(nc.psum_tensor("ps_scores", [P, SBANKS, 512], F32))
        pav = ctx.enter_context(nc.psum_tensor("ps_attended", [P, 2, 512], F32))

        ctx_lo = stream["lo"]
        qk_loaded, v_loaded = sem("qk_loaded"), sem("v_loaded")
        cleared = sem("ident_cleared")
        consts = sem("consts_ready_a")
        proj_done = sem("proj_done")
        proj_hi, proj_lo = sem("proj_hi_ready"), sem("proj_lo_ready")
        maxmm_done, max_done = sem("max_scores_done"), sem("max_done")
        mrow_done, mdiag_done, mb_done, mneg_done = sem("max_rows_done"), sem("max_diag_done"), sem("max_spread"), sem("max_in_queries")
        scores_done, exp_done, p_hi, p_lo = sem("scores_done"), sem("exp_done"), sem("p_hi_ready"), sem("p_lo_ready")
        pv_done = sem("pv_done")
        first_loaded, first_scaled = sem("first_rows_loaded"), sem("first_rows_scaled")
        o_copied, z_inverted = sem("o_copied"), sem("sums_inverted")
        stored = [sem(f"att_stored{i}") for i in range(2)]

        q_d = [s[0:HH].rearrange("(h d) (b q) -> b d h q", d=HD, q=Q) for s in scratch["qk"]]
        k_d = [s[HH:HH + KD].rearrange("(i r) (b q) -> b i r q", r=P, q=Q) for s in scratch["qk"]]
        att_d = scratch["att"].rearrange("(h d) (b q) -> b d h q", d=HD, q=Q)
        rz_d = scratch["rz"].rearrange("h (b q) -> b h q", q=Q)

        with nc.Block() as block:
            @block.sync
            def _(sp):
                for s in stored:
                    sp.sem_inc(s, START)
                def load_qk(b):
                    for i in range(2):
                        sp.dma_start(f(q[i][0:HD, :]).rearrange("d (h q) -> d h q", q=Q), q_d[i][b]).then_inc(qk_loaded, 16)
                        rows = k_d[i][b]
                        sp.dma_start(f(kt[i][0:HD, 0:KTILES, S:SL]),
                                     rows[:, 0:HD].rearrange("i r q -> r i q")).then_inc(qk_loaded, 16)
                        for j in range(KTILES):
                            sp.dma_start(f(kt[i][j * PIECE:(j + 1) * PIECE, KTILES, S:SL]),
                                         rows[j, HD:P]).then_inc(qk_loaded, 16)

                def load_v(b):
                    for i, dst in enumerate((vt_hi[0:Q, NVT, :, 0:HD], vt_lo[0:Q, NVT])):
                        sp.dma_start(f(dst), scratch["v"][i].rearrange("(b q) (h d) -> b q h d", q=Q, d=HD)[b]).then_inc(v_loaded, 16)

                def store_sums(b, h):
                    sp.wait_ge(z_inverted, START + b * H + (h + 1) * G)
                    sp.dma_start(rz_d[bass.ds(b, 1), h * G:(h + 1) * G, :],
                                 osb[HD:HD + 1, h % 2, :].rearrange("d (h q) -> d h q", q=Q)).then_inc(stored[h % 2], 16)

                def store(b, h):
                    sp.wait_ge(o_copied, START + b * KV + h + 1)
                    sp.dma_start(att_d[b, :, h * G:(h + 1) * G, :],
                                 osb[0:HD, h % 2, :].rearrange("d (h q) -> d h q", q=Q)).then_inc(stored[h % 2], 16)
                    if h < KV - 1:
                        store_sums(b, h)

                load_qk(0)
                load_v(0)
                with sp.Fori(0, B - 1) as b:
                    for n in range(LOADS):
                        load_ctx(sp, stream, io, b + 1, n)
                    for h in range(KV):
                        store(b, h)
                    sp.wait_ge(scores_done, b * NU + NU)
                    load_qk(b + 1)
                    sp.wait_ge(pv_done, START + b * NU + NU)
                    load_v(b + 1)
                    store_sums(b, KV - 1)
                for n in range(LOADS):
                    load_wo(sp, stream, io, n)
                for h in range(2):
                    store(B - 1, h)
                for i in range(2):
                    sp.wait_ge(stored[i], START + (B - 1) * 64 + 32)
                sp.wait_ge(stream["lo"], (B + 1) * LOADS)
                load_rows(sp, scratch, 0, *stream["first"], first_loaded)
                for h in range(2, KV):
                    store(B - 1, h)
                store_sums(B - 1, KV - 1)
                for i in range(2):
                    sp.wait_ge(stored[i], START + B * KV // 2 * 32)

            @block.gpsimd
            def _(pool):
                pool.memset(negident[:], 0.0).then_inc(cleared, 1)
                pool.wait_ge(cleared, 1)
                pool.affine_select(out=negident[:], in_=negident[:], compare_op=ALU.not_equal, fill=-1.0, base=0,
                                   pattern=[[-1, HALF]], channel_multiplier=1).then_inc(consts, 1)
                for n, ap in enumerate((ones[:], kt[1][HD:HD + 1], vt_hi[:, :, :, HD:HD + 1])):
                    pool.wait_ge(consts, n + 1)
                    pool.memset(f(ap), 1.0).then_inc(consts, 1)

                with pool.Fori(1, B) as b:
                    for n in range(LOADS):
                        if n % HALVES_C == 0:
                            pool.wait_ge(proj_done, (b - 1) * NPROJ + CHUNKS * KTILES + (n // HALVES_C + 1) * VTC)
                        split_ctx(pool, stream, b, n)
                pool.wait_ge(proj_done, B * NPROJ)
                for n in range(LOADS):
                    split_wo(pool, stream, n)
                pool.wait_ge(first_loaded, ROW_LOADS)
                pool.tensor_tensor(stream["first"][0], stream["first"][0], stream["first"][1], ALU.mult).then_inc(first_scaled, 1)

            @block.scalar
            def _(act):
                for s in (exp_done, o_copied):
                    act.sem_inc(s, START)
                def keys(b, c, i):
                    s = slice(c * CS, (c + 1) * CS)
                    n = c * KTILES + i
                    act.wait_ge(proj_done, b * NPROJ + n + 1)
                    act.copy(kt[0][0:HD, i, s], pproj[n % 2][0:HD, 0:CS]).then_inc(proj_hi, 1)
                    act.copy(kt[0][i * PIECE:(i + 1) * PIECE, KTILES, s], pproj[n % 2][HD:P, 0:CS]).then_inc(proj_hi, 1)

                def values(b, t):
                    n = CHUNKS * KTILES + t
                    act.wait_ge(proj_done, b * NPROJ + n + 1)
                    act.copy(vt_hi[:, t, :, 0:HD], pproj[n % 2][0:VT, 0:KD].rearrange("p (h d) -> p h d", d=HD)).then_inc(proj_hi, 1)

                def exp(b, u):
                    j = u % UNITS
                    R, N = (VT, 2 * GQ) if j < UNITS - 1 else (Q, GQ)
                    act.wait_ge(scores_done, b * NU + u + 1)
                    act.wait_ge(p_lo, START + b * NU + max(u - PRING + 1, 0))
                    act.activation(pr[0:R, u % PRING, 0:N], psc[0:R, u % SBANKS, 0:N], ACT.Exp, scale=SCALE).then_inc(exp_done, 1)

                def probs_hi(b, u):
                    j = u % UNITS
                    R, N = (VT, 2 * GQ) if j < UNITS - 1 else (Q, GQ)
                    act.wait_ge(exp_done, START + b * NU + u + 1)
                    act.wait_ge(pv_done, START + b * NU + max(u - PRING + 1, 0))
                    act.copy(prs[0][0:R, u % PRING, 0:N], pr[0:R, u % PRING, 0:N]).then_inc(p_hi, 1)

                def take_out(b, h):
                    act.wait_ge(pv_done, START + b * NU + (h + 1) * UNITS)
                    act.wait_ge(stored[h % 2], START + b * 64 + 32 * (h // 2))
                    act.copy(osb[0:HD, h % 2, :], pav[0:HD, h % 2, 0:GQ]).then_inc(o_copied, 1)

                with act.Fori(0, B) as b:
                    for c in range(CHUNKS):
                        for i in range(KTILES):
                            keys(b, c, i)
                    for t in range(NVT):
                        values(b, t)
                        if t == NVT - 2:
                            exp(b, 0)
                            probs_hi(b, 0)
                            exp(b, 1)
                        if t == NVT - 3:
                            act.wait_ge(mb_done, b + 1)
                            act.copy(q[0][HD:HD + 1, :], pav[HD:HD + 1, :, 0:KV * HALF]).then_inc(mneg_done, 1)
                    probs_hi(b, 1)
                    for u in range(2, NU):
                        exp(b, u)
                        probs_hi(b, u)
                        if u > UNITS and u % UNITS == AHEAD - 1:
                            take_out(b, u // UNITS - 1)
                    take_out(b, KV - 1)


            @block.vector
            def _(dve):
                for s in (p_lo, proj_lo, max_done, z_inverted):
                    dve.sem_inc(s, START)
                def keys(b, c, i):
                    s = slice(c * CS, (c + 1) * CS)
                    n = c * KTILES + i
                    dve.wait_ge(proj_hi, b * NHI + 2 * n + 1)
                    dve.tensor_tensor(kt[1][0:HD, i, s], pproj[n % 2][0:HD, 0:CS], f(kt[0][0:HD, i, s]), ALU.subtract)
                    piece = slice(i * PIECE, (i + 1) * PIECE)
                    dve.wait_ge(proj_hi, b * NHI + 2 * n + 2)
                    dve.tensor_tensor(kt[1][piece, KTILES, s], pproj[n % 2][HD:P, 0:CS], f(kt[0][piece, KTILES, s]),
                                      ALU.subtract).then_inc(proj_lo, 1)

                def values(b, t):
                    n = CHUNKS * KTILES + t
                    dve.wait_ge(proj_hi, b * NHI + NHI - NVT + t + 1)
                    dve.tensor_tensor(vt_lo[:, t], pproj[n % 2][0:VT, 0:KD].rearrange("p (h d) -> p h d", d=HD),
                                      f(vt_hi[:, t, :, 0:HD]), ALU.subtract).then_inc(proj_lo, 1)

                def part_max(b, p):
                    dve.wait_ge(maxmm_done, b * PARTS + p + 1)
                    N = MAXCOLS[p % 2][1]
                    k = 2 * (p % 2)
                    dve.tensor_reduce(mpart[:, p // 2, p % 2:p % 2 + 1], psc[0:HALF, k:k + 2, 0:N], AX.XY, ALU.max).then_inc(max_done, 1)

                def row_max(b):
                    dve.wait_ge(consts, 4)
                    dve.wait_ge(max_done, START + b * PARTS + PARTS)
                    dve.tensor_tensor(mrow[:], mpart[:, :, 0], mpart[:, :, 1], ALU.max).then_inc(mrow_done, 1)
                    dve.wait_ge(mrow_done, b + 1)
                    for i in range(2):
                        shape = [HALF, KV, HALF]
                        dve.tensor_tensor(mdiag[:, i, :].rearrange("p (a b) -> p a b", a=KV),
                                          negident[:].unsqueeze(1).broadcast_to(shape),
                                          mrow[:, i * KV:(i + 1) * KV].unsqueeze(2).broadcast_to(shape),
                                          ALU.mult).then_inc(mdiag_done, 1)

                def probs_lo(b, u):
                    j = u % UNITS
                    R, N = (VT, 2 * GQ) if j < UNITS - 1 else (Q, GQ)
                    dve.wait_ge(p_hi, b * NU + u + 1)
                    dve.tensor_tensor(prs[1][0:R, u % PRING, 0:N], pr[0:R, u % PRING, 0:N], f(prs[0][0:R, u % PRING, 0:N]),
                                      ALU.subtract).then_inc(p_lo, 1)

                def invert_sums(b, h, g):
                    dve.wait_ge(pv_done, START + b * NU + (h + 1) * UNITS)
                    dve.wait_ge(stored[h % 2], START + b * 64 + 32 * (h // 2))
                    s = slice(g * Q, (g + 1) * Q)
                    dve.reciprocal(osb[HD:HD + 1, h % 2, s], pav[HD:HD + 1, h % 2, s]).then_inc(z_inverted, 1)

                def batch(b, first=False):
                    for c in range(CHUNKS):
                        for i in range(KTILES):
                            keys(b, c, i)
                            n = c * KTILES + i
                            if not first and 2 <= n < 2 + G:
                                invert_sums(b - 1, KV - 1, n - 2)
                    for t in range(NVT):
                        if 2 * t < PARTS:
                            part_max(b, 2 * t)
                        values(b, t)
                        if 2 * t < PARTS:
                            part_max(b, 2 * t + 1)
                        if 2 * t + 2 == PARTS:
                            row_max(b)
                        if t == NVT - 2:
                            probs_lo(b, 0)
                    for u in range(1, NU):
                        probs_lo(b, u)
                        if u > UNITS and 1 <= u % UNITS < 1 + G:
                            invert_sums(b, u // UNITS - 1, u % UNITS - 1)

                batch(0, first=True)
                with dve.Fori(1, B) as b:
                    batch(b)
                for g in range(G):
                    invert_sums(B - 1, KV - 1, g)

            @block.tensor
            def _(pe):
                pe.sem_inc(pv_done, START)
                def project_keys(b, c, i):
                    n = c * KTILES + i
                    if i == 0:
                        pe.wait_ge(ctx_lo, b * LOADS + (c + 1) * HALVES_C)
                    pe.wait_ge(proj_lo, START + b * NPROJ + max(n - 1, 0))
                    for j in range(3 * KT):
                        a, v = TERMS[j % 3]
                        mm = pe.matmul(pproj[n % 2][:, 0:CS], w["wk"][a][:, j // 3, i * P:(i + 1) * P], ct[v][:, c, j // 3, :],
                                       start=(j == 0), stop=(j == 3 * KT - 1))
                    mm.then_inc(proj_done, 1)

                def project_values(b, t, part):
                    n = CHUNKS * KTILES + t
                    if part == 0:
                        pe.wait_ge(proj_lo, START + b * NPROJ + n - 1)
                    s = slice(t % VTC * VT, (t % VTC + 1) * VT)
                    half = 3 * KT // 2
                    for j in range(part * half, part * half + half):
                        a, v = TERMS[j % 3]
                        mm = pe.matmul(pproj[n % 2][0:VT, 0:KD], ct[a][:, t // VTC, j // 3, s], w["wv"][v][:, j // 3, :],
                                       start=(j == 0), stop=(j == 3 * KT - 1))
                    if part == 1:
                        mm.then_inc(proj_done, 1)

                def max_scores(b, p):
                    if p == 0:
                        pe.wait_ge(qk_loaded, b * 160 + 160)
                        pe.wait_ge(exp_done, START + b * NU)
                    pe.wait_ge(max_done, START + b * PARTS + max(p - 1, 0))
                    h = p // 2
                    first, N = MAXCOLS[p % 2]
                    for i in range(2):
                        mm = pe.matmul(psc[0:HALF, 2 * (p % 2) + i, 0:N], q[0][0:HD, h * HALF:(h + 1) * HALF],
                                       kt[0][:, h // 2, first + i * N:first + (i + 1) * N], start=True, stop=True)
                    mm.then_inc(maxmm_done, 1)

                def spread_max(b):
                    pe.wait_ge(mdiag_done, 2 * b + 2)
                    pe.wait_ge(o_copied, START + b * KV)
                    pe.wait_ge(z_inverted, START + b * H)
                    for i in range(2):
                        mm = pe.matmul(pav[:, i, 0:KV * HALF], ones[:], mdiag[:, i, :], start=True, stop=True)
                    mm.then_inc(mb_done, 1)

                def scores(b, u):
                    h, j = u // UNITS, u % UNITS
                    if u < SBANKS:
                        pe.wait_ge(max_done, START + b * PARTS + PARTS)
                    else:
                        pe.wait_ge(exp_done, START + b * NU + u - SBANKS + 1)
                    tiles = (2 * j, 2 * j + 1) if j < UNITS - 1 else (NVT,)
                    for n, t in enumerate(tiles):
                        s = slice(t * VT, min((t + 1) * VT, SL))
                        R = s.stop - s.start
                        o = psc[0:R, u % SBANKS, n * GQ:(n + 1) * GQ]
                        c = slice(h * GQ, (h + 1) * GQ)
                        pe.matmul(o, kt[0][:, h, s], q[0][0:HD, c], start=True, stop=False)
                        pe.matmul(o, kt[0][:, h, s], q[1][:, c], start=False, stop=False)
                        if u == 0 and n == 0:
                            pe.wait_ge(mneg_done, b + 1)
                        mm = pe.matmul(o, kt[1][:, h, s], q[0][:, c], start=False, stop=True)
                    mm.then_inc(scores_done, 1)

                def weigh(b, u):
                    h, j = u // UNITS, u % UNITS
                    pe.wait_ge(p_lo, START + b * NU + u + 1)
                    if u == 0:
                        pe.wait_ge(v_loaded, b * 32 + 32)
                    if h == 0 and j < UNITS - 1:
                        pe.wait_ge(proj_lo, START + b * NPROJ + CHUNKS * KTILES + 2 * j + 2)
                    if j == 0 and h >= 2:
                        pe.wait_ge(o_copied, START + b * KV + h - 1)
                        pe.wait_ge(z_inverted, START + b * H + (h - 1) * G)
                    tiles = (2 * j, 2 * j + 1) if j < UNITS - 1 else (NVT,)
                    for n, t in enumerate(tiles):
                        R = VT if t < NVT else Q
                        c = slice(n * GQ, (n + 1) * GQ)
                        o = pav[0:HD + 1, h % 2, 0:GQ]
                        hi, lo = (x[0:R, u % PRING, c] for x in prs)
                        pe.matmul(o, vt_hi[0:R, t, h], hi, start=(t == 0), stop=False)
                        pe.matmul(pav[0:HD, h % 2, 0:GQ], vt_lo[0:R, t, h], hi, start=False, stop=False)
                        mm = pe.matmul(o, vt_hi[0:R, t, h], lo, start=False, stop=(t == NVT))
                    mm.then_inc(pv_done, 1)

                with pe.Fori(0, B) as b:
                    for c in range(CHUNKS):
                        for i in range(KTILES):
                            project_keys(b, c, i)
                    for t in range(NVT):
                        for part in range(2):
                            project_values(b, t, part)
                            if 2 * t + part < PARTS:
                                max_scores(b, 2 * t + part)
                        if t == NVT - 3:
                            spread_max(b)
                        if t == NVT - 2:
                            scores(b, 0)
                            scores(b, 1)
                    for u in range(2, AHEAD):
                        scores(b, u)
                    for u in range(NU):
                        if u + AHEAD < NU:
                            scores(b, u + AHEAD)
                        weigh(b, u)


def combine(nc, stream, early, io, scratch):
    with ExitStack() as ctx:
        sb = lambda name, shape, dt=F32: ctx.enter_context(nc.sbuf_tensor(name, shape, dt))
        sem = lambda name: ctx.enter_context(nc.semaphore(name))
        wg = sb("w_gate", [P, KT, E])
        bg = sb("b_gate", [1, E])
        ones = sb("ones_g", [1, P])
        ident = sb("ident_g", [P, P])
        iota_u = sb("iota_u", [P, E], mybir.dt.int32)
        iota = sb("iota_f", [P, E])
        eps = sb("eps_g", [P, 1])
        wo = stream["wo"]
        att, rz = ([first, sb(name, [P, HT, P])[:]] for first, name in zip(stream["first"], ("att", "inv_sums")))
        an = sb("att_scaled", [P, HT, P])
        ats = [sb(f"att_{n}", [P, 2, HT, P], F32R) for n in ("hi", "lo")]
        x = sb("x_rows", [P, 2, D])
        x1 = sb("x1", [P, 2, D + E])
        stats, mv, std, rstd = sb("stats_g", [P, 6]), sb("mv_g", [P, 2]), sb("std_g", [P, 1]), sb("rstd_g", [P, 1])
        xn = sb("xn_g", [P, D])
        xt = sb("xt_g", [P, 2, KT, P])
        lg = sb("logits", [P, E])
        top, topi = sb("top", [P, E]), sb("top_index", [P, E], U32)
        topf = sb("top_index_f", [P, E])
        sel = sb("selected", [P, 2, E])
        po = [ctx.enter_context(nc.psum_tensor(f"ps_o{i}", [P, D], F32)) for i in range(2)]
        pt = ctx.enter_context(nc.psum_tensor("ps_t", [P, KT, P], F32))
        pg = ctx.enter_context(nc.psum_tensor("ps_g", [P, E], F32))

        loaded = [sem(f"rows_loaded{i}") for i in range(2)]
        x_loaded = [sem(f"x_rows_loaded{i}") for i in range(2)]
        small_loaded, consts = sem("small_loaded"), sem("consts_g")
        scaled, a_hi, a_lo = sem("att_scaled_done"), sem("att_hi_ready"), sem("att_lo_ready")
        o_done, x1_done = sem("o_done"), sem("x1_done")
        waited, waited_pool = sem("waited_g"), sem("waited_pool_g")
        stats_done, aggregated, std_done, rstd_done = sem("stats_done_g"), sem("aggregated"), sem("std_done_g"), sem("rstd_done_g")
        normed = sem("normed_g")
        logits_ready, top_ready, index_ready = sem("logits_ready"), sem("top_ready"), sem("index_ready")
        index_f_ready, sel_ready = sem("index_f_ready"), sem("sel_ready")
        turned, xt_done, g_done, gate_done = sem("turned_g"), sem("xt_ready"), sem("gate_logits"), sem("gate_done")
        stored = [sem(f"rows_stored{i}") for i in range(2)]
        x_v = io["x"].rearrange("(t r) d -> t r d", r=P)
        e_loaded = [sem(f"expert_half_loaded{i}") for i in range(2)]
        e_hi, e_lo = sem("expert_half_hi"), sem("expert_half_lo")
        first_hi, first_lo = sem("first_tile_hi"), sem("first_tile_lo")

        with nc.Block() as block:
            @block.sync
            def _(sp):
                for s in stored:
                    sp.sem_inc(s, START)
                def load(t, s):
                    load_rows(sp, scratch, t, att[s], rz[s], loaded[s])

                def load_expert(j):
                    e, n = j // 2, j % 2
                    k = slice(n * KH, (n + 1) * KH)
                    if e == EARLY + 1:
                        sp.wait_ge(e_lo, 2)
                    sp.dma_start(early["raw"][:, e % 2, k], io["we"][:, e, k, :]).then_inc(
                        e_loaded[n] if e < EARLY else early["loaded"][e % 2], 16)

                def load_x(t, s):
                    sp.dma_start(x[:, s], x_v[t]).then_inc(x_loaded[s], 16)

                def store(t, s):
                    sp.wait_ge(xt_done, t + 1)
                    sp.dma_start(scratch["xt"][t], xt[:, s]).then_inc(stored[s], 16)
                    sp.wait_ge(gate_done, t + 1)
                    sp.dma_start(scratch["x1"][t], x1[:, s]).then_inc(stored[s], 16)

                load(1, 1)
                load_x(0, 0)
                sp.dma_start(wg[:], io["wg"]).then_inc(small_loaded, 16)
                sp.dma_start(bg[:], io["bg"]).then_inc(small_loaded, 16)
                sp.dma_start(early["be"][:], io["be"]).then_inc(early["be_loaded"], 16)
                load_x(1, 1)

                def tile(t, s, more=True, first=False):
                    if more:
                        if first:
                            sp.wait_ge(a_lo, START + 1)
                        else:
                            sp.wait_ge(scaled, t + 1)
                        load(t + 2, s)
                        sp.wait_ge(x1_done, t + 1)
                        load_x(t + 2, s)
                    if not first:
                        store(t - 1, 1 - s)

                tile(0, 0, first=True)
                for i in range(OT // 2 - 2):
                    for s in (1, 0):
                        tile(2 * i + 2 - s, s)
                    load_expert(i)
                tile(OT - 3, 1)
                load_expert(OT // 2 - 2)
                tile(OT - 2, 0, more=False)
                sp.wait_ge(stored[0], START + 32 * (OT // 2 - 1))
                load_normed(sp, scratch, early, 0, 0)
                tile(OT - 1, 1, more=False)
                store(OT - 1, 1)
                for s in range(2):
                    sp.wait_ge(stored[s], START + 32 * OT // 2)

            @block.gpsimd
            def _(pool):
                pool.memset(eps[:], EPS).then_inc(consts, 1)
                pool.memset(ones[:], 1.0).then_inc(consts, 1)
                pool.memset(ident[:], 0.0).then_inc(consts, 1)
                pool.iota(iota_u[:], pattern=[[1, E]], base=0, channel_multiplier=0).then_inc(consts, 1)
                pool.wait_ge(consts, 4)
                pool.affine_select(out=ident[:], in_=ident[:], compare_op=ALU.not_equal, fill=1.0, base=0,
                                   pattern=[[-1, P]], channel_multiplier=1).then_inc(consts, 1)
                pool.tensor_copy(iota[:], iota_u[:]).then_inc(consts, 1)

                pool.sem_inc(scaled, 1)

                def scale(i, s):
                    pool.wait_ge(loaded[s], (i + s) * ROW_LOADS)
                    pool.wait_ge(a_lo, START + 2 * i + s)
                    pool.tensor_tensor(an[:], att[s], rz[s], ALU.mult).then_inc(scaled, 1)

                def split_half(e, n):
                    k = slice(n * KH, (n + 1) * KH)
                    raw, (hi, lo) = early["raw"][:, 0, k], (p[:, e, k] for p in early["parts"])
                    wait_apart(pool, e_loaded[n], 16 * e + 16, waited_pool)
                    pool.tensor_scalar(hi, raw, 1.0, 0.0, ALU.mult, ALU.add).then_inc(e_hi, 1)
                    pool.wait_ge(e_hi, 2 * e + n + 1)
                    pool.tensor_tensor(lo, raw, f(hi), ALU.subtract).then_inc(e_lo, 1)

                scale(0, 1)
                with pool.Fori(1, SPLIT_TILES[0] // 2) as i:
                    for s in range(2):
                        scale(i, s)
                for n, t in enumerate(SPLIT_TILES):
                    scale(t // 2, t % 2)
                    split_half(0, n)
                with pool.Fori(SPLIT_TILES[0] // 2 + 1, OT // 2) as i:
                    for s in range(2):
                        scale(i, s)
                wait_apart(pool, early["tile_loaded"][0], 32, waited_pool)
                hi, lo = (x[:, 0] for x in early["xs"])
                pool.tensor_scalar(hi, early["xt"][:, 0], 1.0, 0.0, ALU.mult, ALU.add).then_inc(first_hi, 1)
                pool.wait_ge(first_hi, 1)
                pool.tensor_tensor(lo, early["xt"][:, 0], f(hi), ALU.subtract).then_inc(first_lo, 1)

            @block.scalar
            def _(act):
                def split(t, s):
                    act.wait_ge(scaled, t + 1)
                    act.wait_ge(o_done, START + t - 1)
                    act.copy(ats[0][:, s], an[:]).then_inc(a_hi, 1)

                def deviation(t):
                    act.wait_ge(aggregated, t + 1)
                    act.activation(std[:], mv[:, 1:2], ACT.Sqrt, bias=eps[:]).then_inc(std_done, 1)

                def turn(t, s):
                    act.wait_ge(turned, START + t + 1)
                    act.wait_ge(stored[s], START + (t - s) * 16)
                    act.copy(xt[:, s], pt[:]).then_inc(xt_done, 1)

                def finish(t, s, more):
                    deviation(t)
                    if more:
                        split(t + 2, s)
                    turn(t, s)

                act.copy(ats[0][:, 0], att[0]).then_inc(a_hi, 1)
                split(1, 1)
                act.wait_ge(consts, 6)
                with act.Fori(0, OT // 2 - 1) as i:
                    for s in range(2):
                        finish(2 * i + s, s, True)
                for s in range(2):
                    finish(OT - 2 + s, s, False)

            @block.vector
            def _(dve):
                for s in (a_lo, logits_ready):
                    dve.sem_inc(s, START)
                def split(t, s, src):
                    dve.wait_ge(a_hi, t + 1)
                    dve.tensor_tensor(ats[1][:, s], src, f(ats[0][:, s]), ALU.subtract).then_inc(a_lo, 1)

                def norm(t, s):
                    dve.wait_ge(o_done, START + t + 1)
                    dve.wait_ge(x_loaded[s], (t - s) * 8 + 16)
                    dve.wait_ge(stored[s], START + (t - s) * 16)
                    dve.tensor_tensor(x1[:, s, 0:D], po[s][:], x[:, s], ALU.add).then_inc(x1_done, 1)
                    dve.wait_ge(x1_done, t + 1)
                    dve.bn_stats(stats[:], x1[:, s, 0:D]).then_inc(stats_done, 1)
                    wait_apart(dve, stats_done, t + 1, waited)
                    dve.bn_aggr(mv[:], stats[:]).then_inc(aggregated, 1)
                    dve.wait_ge(std_done, t + 1)
                    dve.reciprocal(rstd[:], std[:]).then_inc(rstd_done, 1)
                    dve.wait_ge(rstd_done, t + 1)
                    dve.wait_ge(turned, START + t)
                    dve.tensor_scalar(xn[:], x1[:, s, 0:D], mv[:, 0:1], rstd[:], ALU.subtract, ALU.mult).then_inc(normed, 1)

                def gate(t, s):
                    dve.wait_ge(g_done, t + 1)
                    dve.tensor_copy(lg[:], pg[:]).then_inc(logits_ready, 1)
                    wait_apart(dve, logits_ready, START + t + 1, waited)
                    dve.max(top[:], lg[:]).then_inc(top_ready, 1)
                    wait_apart(dve, top_ready, t + 1, waited)
                    dve.max_index(topi[:], top[:], lg[:]).then_inc(index_ready, 1)
                    dve.wait_ge(index_ready, t + 1)
                    dve.tensor_copy(topf[:], topi[:]).then_inc(index_f_ready, 1)
                    dve.wait_ge(index_f_ready, t + 1)
                    for n in range(2):
                        dve.tensor_scalar(sel[:, n, :], iota[:], topf[:, n:n + 1], 0.5, ALU.is_equal, ALU.mult).then_inc(sel_ready, 1)
                    dve.wait_ge(sel_ready, 2 * t + 2)
                    dve.tensor_tensor(x1[:, s, D:D + E], sel[:, 0, :], sel[:, 1, :], ALU.add).then_inc(gate_done, 1)

                def finish(t, s, more):
                    norm(t, s)
                    if more:
                        split(t + 2, s, an[:])
                    gate(t, s)

                split(0, 0, att[0])
                split(1, 1, an[:])
                dve.wait_ge(consts, 6)
                with dve.Fori(0, OT // 2 - 1) as i:
                    for s in range(2):
                        finish(2 * i + s, s, True)
                for s in range(2):
                    finish(OT - 2 + s, s, False)

            @block.tensor
            def _(pe):
                for s in (o_done, turned):
                    pe.sem_inc(s, START)

                def turn(t):
                    pe.wait_ge(normed, t + 1)
                    for k in range(KT):
                        mm = pe.transpose(pt[:, k, :], xn[:, k * P:(k + 1) * P], ident[:])
                    mm.then_inc(turned, 1)

                def logits(t, s):
                    pe.wait_ge(xt_done, t + 1)
                    pe.wait_ge(logits_ready, START + t)
                    for k in range(KT):
                        pe.matmul(pg[:], xt[:, s, k, :], wg[:, k, :], start=(k == 0), stop=False)
                    pe.matmul(pg[:], ones[:], bg[:], start=False, stop=True).then_inc(g_done, 1)

                def output(t, s, first=False):
                    pe.wait_ge(a_lo, START + t + 1)
                    n = 3 * HT
                    for j in range(n):
                        mm = pe.matmul(po[s][:], ats[TERMS[j % 3][0]][:, s, j // 3, :], wo[TERMS[j % 3][1]][:, j // 3, :],
                                       start=(j == 0), stop=(j == n - 1))
                        if not first and j == n // 2:
                            turn(t - 1)
                        if not first and j == 3 * n // 4:
                            logits(t - 1, 1 - s)
                    mm.then_inc(o_done, 1)

                output(0, 0, first=True)
                pe.wait_ge(consts, 6)
                pe.wait_ge(small_loaded, 32)
                with pe.Fori(0, OT // 2 - 1) as i:
                    for s in (1, 0):
                        output(2 * i + 2 - s, s)
                output(OT - 1, 1)
                turn(OT - 1)
                logits(OT - 1, 1)


def experts(nc, stream, early, io, scratch, out_d):
    with ExitStack() as ctx:
        sb = lambda name, shape, dt=F32: ctx.enter_context(nc.sbuf_tensor(name, shape, dt))
        sem = lambda name: ctx.enter_context(nc.semaphore(name))
        BANKS, YRING = 4, 2
        w_loaded = early["loaded"]
        third = stream["raw_full"][:].rearrange("p n c -> p (n c)")[:, 0:KT * D].rearrange("p (k d) -> p k d", d=D)
        raws = [early["raw"][:, 0], early["raw"][:, 1], third]
        slot = lambda e: (1, 0, 2)[(e - EARLY) % RAW_E]
        count = lambda e: 16 * ((e - EARLY) // RAW_E + 1) + (16 if slot(e) < 2 else 0)
        we = [[t[:, e] for e in range(EARLY)] for t in early["parts"]]
        for n, home in enumerate(stream["wo"]):
            we[n] += [home[:, e * KT:(e + 1) * KT] for e in range(HT // KT)]
            last = sb(f"we_last_{n}", [P, LATE - HT // KT, KT, D], F32R)
            we[n] += [last[:, e] for e in range(LATE - HT // KT)]
        be_raw, b_loaded = early["be"], early["be_loaded"]
        be_lo = sb("be_lo", [E, D], F32R)
        be = sb("be", [2 * E, D], F32R)
        pick_f = stream["raw_full"][0:2 * E, 2:3, :].rearrange("p n (e r) -> p (n e) r", r=P)
        pick = sb("pick", [2 * E, E, P], F32R)
        bias = sb("bias", [P, E, D])
        xt, xs, x1, loaded = (early[n] for n in ("xt", "xs", "x1", "tile_loaded"))
        y = sb("y", [P, YRING, D])
        acc = sb("acc", [P, 2, D])
        po = [ctx.enter_context(nc.psum_tensor(f"ps_e{i}", [P, D], F32)) for i in range(BANKS)]
        pb = [ctx.enter_context(nc.psum_tensor(f"ps_bias{i}", [P, D], F32)) for i in range(BANKS)]

        b_moved = sem("be_moved")
        consts = sem("consts_e")
        w_hi, w_lo, b_hi, b_lo = sem("we_hi_ready"), sem("we_lo_ready"), sem("be_hi_ready"), sem("be_lo_ready")
        x_hi, x_lo = sem("xs_hi_ready"), sem("xs_lo_ready")
        spread, bias_ready, biased = sem("bias_spread"), sem("bias_ready"), sem("biased")
        e_done, relu_done, acc_done = sem("expert_done"), sem("relu_done"), sem("acc_done")
        stored = [sem(f"out_stored{i}") for i in range(2)]
        out_v = out_d.rearrange("(t r) d -> t r d", r=P)

        with nc.Block() as block:
            @block.sync
            def _(sp):
                for s in stored:
                    sp.sem_inc(s, START)
                def load(t, s):
                    load_normed(sp, scratch, early, t, s)

                sp.wait_ge(b_lo, 1)
                sp.dma_start(f(be[E:2 * E, :]), f(be_lo[:])).then_inc(b_moved, 16)
                for e in range(EARLY + 2, E):
                    if e >= EARLY + RAW_E:
                        sp.wait_ge(w_lo, e - EARLY - RAW_E + 1)
                    sp.dma_start(raws[slot(e)], io["we"][:, e]).then_inc(w_loaded[slot(e)], 16)
                    if e == EARLY + 2:
                        load(1, 1)

                def tile(t, s, more):
                    sp.wait_ge(acc_done, YRING + t * E + E)
                    if more:
                        load(t + 2, s)
                    sp.dma_start(out_v[t], acc[:, s]).then_inc(stored[s], 16)

                with sp.Fori(0, OT // 2 - 1) as i:
                    for s in range(2):
                        tile(2 * i + s, s, True)
                for s in range(2):
                    tile(OT - 2 + s, s, False)
                for s in range(2):
                    sp.wait_ge(stored[s], START + 16 * OT // 2)

            @block.gpsimd
            def _(pool):
                pool.memset(pick_f[:], 0.0).then_inc(consts, 1)
                for n in range(2):
                    pool.wait_ge(consts, n + 1)
                    pool.affine_select(out=pick_f[:], in_=pick_f[:], compare_op=ALU.not_equal, fill=1.0, base=-E * n,
                                       pattern=[[-1, E], [0, P]], channel_multiplier=1).then_inc(consts, 1)

            @block.scalar
            def _(act):
                def split(t, i, s):
                    act.wait_ge(loaded[s], i * 32 + 32)
                    act.copy(xs[0][:, s], xt[:, s]).then_inc(x_hi, 1)

                def split_w(e):
                    act.wait_ge(w_loaded[slot(e)], count(e))
                    act.copy(we[0][e], raws[slot(e)]).then_inc(w_hi, 1)

                act.sem_inc(x_hi, 1)
                act.wait_ge(b_loaded, 16)
                act.copy(be[0:E, :], be_raw[:]).then_inc(b_hi, 1)
                split_w(EARLY)
                split_w(EARLY + 1)

                def tile(i, s, more, first=False):
                    t = 2 * i + s
                    for e in range(E):
                        if first and e % BANKS == 0:
                            for n in range(e, e + BANKS):
                                act.wait_ge(spread, n + 1)
                                act.copy(bias[:, n, :], pb[n % BANKS][:]).then_inc(bias_ready, 1)
                        act.wait_ge(biased, BANKS + t * E + e + 1)
                        act.activation(y[:, e % YRING], y[:, e % YRING], ACT.Relu, scale=x1[:, s, D + e:D + e + 1]).then_inc(relu_done, 1)
                        if first and EARLY + 2 <= e + 3 < E:
                            split_w(e + 3)
                        if e == 2 and more:
                            split(t + 1, i + s, 1 - s)

                for s in range(2):
                    tile(0, s, True, first=(s == 0))
                with act.Fori(1, OT // 2 - 1) as i:
                    for s in range(2):
                        tile(i, s, True)
                for s in range(2):
                    tile(OT // 2 - 1, s, s == 0)

            @block.vector
            def _(dve):
                dve.sem_inc(acc_done, YRING)
                dve.sem_inc(biased, BANKS)
                def split(t, s):
                    dve.wait_ge(x_hi, t + 1)
                    dve.tensor_tensor(xs[1][:, s], xt[:, s], f(xs[0][:, s]), ALU.subtract).then_inc(x_lo, 1)

                dve.sem_inc(x_lo, 1)

                def split_w(e):
                    dve.wait_ge(w_hi, e - EARLY + 1)
                    dve.tensor_tensor(we[1][e], raws[slot(e)], f(we[0][e]), ALU.subtract).then_inc(w_lo, 1)

                dve.wait_ge(b_hi, 1)
                dve.tensor_tensor(be_lo[:], be_raw[:], f(be[0:E, :]), ALU.subtract).then_inc(b_lo, 1)
                split_w(EARLY)
                dve.wait_ge(consts, 3)
                dve.tensor_copy(pick[:], pick_f[:]).then_inc(consts, 1)
                split_w(EARLY + 1)

                def add_up(t, e, s):
                    dve.wait_ge(relu_done, t * E + e + 1)
                    dve.wait_ge(acc_done, YRING + t * E + e)
                    dve.tensor_tensor(acc[:, s], x1[:, s, 0:D] if e == 0 else acc[:, s], y[:, e % YRING], ALU.add).then_inc(acc_done, 1)

                def tile(i, s, more, first=False):
                    t = 2 * i + s
                    dve.wait_ge(stored[s], START + 16 * i)
                    for e in range(E + 1):
                        if e < E:
                            if first:
                                dve.wait_ge(bias_ready, e + 1)
                            dve.wait_ge(e_done, t * E + e + 1)
                            dve.wait_ge(acc_done, t * E + e + 1)
                            dve.tensor_tensor(y[:, e % YRING], po[e % BANKS][:], bias[:, e, :], ALU.add).then_inc(biased, 1)
                        if e > 0:
                            add_up(t, e - 1, s)
                            if first and EARLY + 2 <= e + 2 < E:
                                split_w(e + 2)
                        if e == 3 and more:
                            split(t + 1, 1 - s)

                for s in range(2):
                    tile(0, s, True, first=(s == 0))
                with dve.Fori(1, OT // 2 - 1) as i:
                    for s in range(2):
                        tile(i, s, True)
                for s in range(2):
                    tile(OT // 2 - 1, s, s == 0)

            @block.tensor
            def _(pe):
                def tile(i, s, first=False):
                    t = 2 * i + s
                    pe.wait_ge(x_lo, t + 1)
                    for e in range(E):
                        if e >= EARLY:
                            pe.wait_ge(w_lo, e - EARLY + 1)
                        pe.wait_ge(biased, t * E + e + 1)
                        for j in range(3 * KT):
                            a, v = TERMS[j % 3]
                            mm = pe.matmul(po[e % BANKS][:], xs[a][:, s, j // 3, :], we[v][e][:, j // 3, :],
                                           start=(j == 0), stop=(j == 3 * KT - 1))
                        mm.then_inc(e_done, 1)
                        if first and e % 3 == 0 and e // 3 < E // BANKS:
                            pe.wait_ge(b_moved, 16)
                            pe.wait_ge(consts, 4)
                            for n in range(e // 3 * BANKS, (e // 3 + 1) * BANKS):
                                if n >= BANKS:
                                    pe.wait_ge(bias_ready, n - BANKS + 1)
                                pe.matmul(pb[n % BANKS][:], pick[:, n, :], be[:], start=True, stop=True).then_inc(spread, 1)

                for s in range(2):
                    tile(0, s, first=(s == 0))
                with pe.Fori(1, OT // 2) as i:
                    for s in range(2):
                        tile(i, s)


def build(nc, io, out_d):
    scratch = {
        "qk": [nc.dram_tensor(f"qk_{n}", (HH + KD, ROWS), F32, kind="Internal").ap() for n in ("hi", "lo")],
        "v": [nc.dram_tensor(f"v_{n}", (ROWS, KD), F32, kind="Internal").ap() for n in ("hi", "lo")],
        "att": nc.dram_tensor("att_t", (HH, ROWS), F32, kind="Internal").ap(),
        "rz": nc.dram_tensor("inverse_sums", (H, ROWS), F32, kind="Internal").ap(),
        "x1": nc.dram_tensor("x1_gate", (OT, P, D + E), F32, kind="Internal").ap(),
        "xt": nc.dram_tensor("xt_normed", (OT, P, KT * P), F32, kind="Internal").ap(),
    }
    scratch["xt"] = scratch["xt"].rearrange("t p (k r) -> t p k r", k=KT)
    with ExitStack() as ctx:
        parts = ctx.enter_context(nc.sbuf_tensor("parts", [P, 2, HT * D], F32R))
        wo = [parts[:, i].rearrange("p (t d) -> p t d", d=D) for i in range(2)]
        raw = ctx.enter_context(nc.sbuf_tensor("raw", [P, RAW, WOT * D], F32))
        sem = lambda name: ctx.enter_context(nc.semaphore(name))
        stream = {
            "raw_full": raw, "first": [raw[:].rearrange("p n c -> p (n c)")[:, i * HH:(i + 1) * HH]
                                       .rearrange("p (k r) -> p k r", r=P) for i in range(2)],
            "raw": raw[:, :, 0:KH * CS].rearrange("p n (k s) -> p n k s", s=CS), "wo": wo,
            "parts": [parts[:, i, 0:CHUNKS * KT * CS].rearrange("p (c k s) -> p c k s", c=CHUNKS, k=KT) for i in range(2)],
            "loaded": [sem(f"ctx_loaded{i}") for i in range(RAW)],
            "hi": sem("ctx_hi_ready"), "lo": sem("ctx_lo_ready"), "waited": sem("ctx_waited"),
        }
        with ExitStack() as inner:
            w = {name: [inner.enter_context(nc.sbuf_tensor(f"{name}_{n}", [P, KT, KD], F32R)) for n in ("hi", "lo")]
                 for name in ("wk", "wv")}
            project(nc, w, stream, io, scratch)
            attend(nc, w, stream, io, scratch)
        early = {
            "raw": ctx.enter_context(nc.sbuf_tensor("we_raw", [P, 2, KT, D], F32)),
            "parts": [ctx.enter_context(nc.sbuf_tensor(f"we_early_{n}", [P, EARLY, KT, D], F32R)) for n in ("hi", "lo")],
            "loaded": [sem(f"we_loaded{i}") for i in range(RAW_E)],
            "xt": ctx.enter_context(nc.sbuf_tensor("xt_e", [P, 2, KT, P], F32)),
            "xs": [ctx.enter_context(nc.sbuf_tensor(f"xs_{n}", [P, 2, KT, P], F32R)) for n in ("hi", "lo")],
            "x1": ctx.enter_context(nc.sbuf_tensor("x1_e", [P, 2, D + E], F32)),
            "be": ctx.enter_context(nc.sbuf_tensor("be_raw", [E, D], F32)), "be_loaded": sem("be_loaded"),
            "tile_loaded": [sem(f"tile_loaded{i}") for i in range(2)],
        }
        combine(nc, stream, early, io, scratch)
        experts(nc, stream, early, io, scratch, out_d)


def kernel(x, ctx_4096, L0_xattn_Wq, L0_xattn_Wk, L0_xattn_Wv, L0_xattn_Wo, L0_ffn_W_gate, L0_ffn_b_gate,
           L0_ffn_W_e, L0_ffn_b_e):
    import numpy as np
    import concourse.bacc as bacc
    from concourse.bass_utils import run_bass_kernel_spmd

    def stationary(w):
        return w.T.reshape(-1, P, w.shape[0]).transpose(1, 0, 2)

    wk = np.asarray(L0_xattn_Wk)
    last = wk[KTILES * HD:]
    wk_tiles = np.concatenate([part for i in range(KTILES)
                               for part in (wk[i * HD:(i + 1) * HD], last[i * PIECE:(i + 1) * PIECE])])
    arrays = {
        "x": np.asarray(x).reshape(ROWS, D),
        "ctx": np.asarray(ctx_4096).reshape(B, CHUNKS, CS, KT, P).transpose(0, 1, 4, 3, 2),
        "wq": stationary(np.asarray(L0_xattn_Wq)),
        "wk": stationary(wk_tiles),
        "wv": stationary(np.asarray(L0_xattn_Wv)),
        "wo": stationary(np.asarray(L0_xattn_Wo)),
        "wg": np.asarray(L0_ffn_W_gate).reshape(KT, P, E).transpose(1, 0, 2),
        "bg": np.asarray(L0_ffn_b_gate).reshape(1, E),
        "we": np.asarray(L0_ffn_W_e).reshape(E, KT, P, D).transpose(2, 0, 1, 3),
        "be": np.asarray(L0_ffn_b_e),
    }
    arrays = {k: np.ascontiguousarray(v) for k, v in arrays.items()}
    nc = bacc.Bacc("TRN2", target_bir_lowering=False, num_devices=1)
    io = {k: nc.dram_tensor(f"in_{k}", v.shape, F32, kind="ExternalInput").ap() for k, v in arrays.items()}
    out_d = nc.dram_tensor("out", (ROWS, D), F32, kind="ExternalOutput").ap()
    build(nc, io, out_d)
    r = run_bass_kernel_spmd(nc, [{f"in_{k}": v for k, v in arrays.items()}], core_ids=[0])
    return r.results[0]["out"].reshape(B, Q, D)
```
